# Optimizing a Trainium2 kernel written in Bass

```python
import numpy as np
import jax
import jax.numpy as jnp

def _softmax(x, axis=-1):
    return jax.nn.softmax(x, axis=axis)

def _gelu(x):
    return jax.nn.gelu(x, approximate=True)

def _silu(x):
    return jax.nn.silu(x)

def _sigmoid(x):
    return jax.nn.sigmoid(x)

def _layernorm(x, axis=-1, eps=1e-05):
    m = jnp.mean(x, axis=axis, keepdims=True)
    v = jnp.var(x, axis=axis, keepdims=True)
    return (x - m) / jnp.sqrt(v + eps)

def _scatter_add(tgt, idx, src, axis=0):
    return tgt.at[idx].add(src)

def _segment_sum(src, seg, n):
    return jax.ops.segment_sum(src, seg, n)
kernel_name = 'mk_xattn_ffn_d1_seqx_r4_d51156'

def setup_inputs(seed: int=0):
    np.random.seed(seed)
    _w = jnp.asarray

    def _rec_inputs():
        import jax
        import jax.numpy as jnp
        _rk = jax.random.key(seed)
        x = -0.0002928 + 1 * jax.random.normal(jax.random.fold_in(_rk, 1), (16, 256, 256), jnp.float32)
        _lenS = 256 - jax.random.randint(jax.random.fold_in(_rk, 7), (16,), 0, max(1, 256 // 4) + 1, jnp.int32)
        _lenS2 = 256 - jax.random.randint(jax.random.fold_in(_rk, 8), (16,), 0, max(1, 256 // 4) + 1, jnp.int32)
        _ctx_1024P = jax.random.normal(jax.random.fold_in(_rk, 11), (16, 16, 256), jnp.float32)
        _ctx_1024c = jax.random.dirichlet(jax.random.fold_in(_rk, 511), 0.3 * jnp.ones((16,), jnp.float32), (16, 256))
        _ctx_1024t = jnp.einsum('bsk,bkd->bsd', _ctx_1024c, _ctx_1024P)
        _ctx_1024t = _ctx_1024t * jax.lax.rsqrt(jnp.mean(jnp.square(_ctx_1024t)) + 1e-12) * 0.953939
        ctx_1024 = -1.39393e-06 + 0.999914 * (_ctx_1024t + 0.3 * jax.random.normal(jax.random.fold_in(_rk, 611), (16, 256, 256), jnp.float32))
        _validS = jnp.arange(256)[None, :] < _lenS[:, None]
        _validS2 = jnp.arange(256)[None, :] < _lenS2[:, None]
        _causal = jnp.tril(jnp.ones((256, 256), dtype=bool))
        mask_Bx1x1xS2_ik0 = jnp.where(jnp.broadcast_to(_validS2[:, None, None, :], (16, 1, 1, 256)), 0, 1).astype(jnp.int32)
        return (x, ctx_1024, mask_Bx1x1xS2_ik0)
    x, ctx_1024, mask_Bx1x1xS2_ik0 = _rec_inputs()

    def _L0_xattn_setup():
        import jax, jax.numpy as jnp
        import numpy as np
        B, S, D, H = (2, 512, 256, 16)
        DEPTH = D // H

        def _split_heads(x):
            b, s, _ = x.shape
            return x.reshape(b, s, H, DEPTH).transpose(0, 2, 1, 3)
        key = jax.random.key(seed)
        ks = jax.random.split(key, 12)
        inp = {'query': jax.random.normal(ks[0], (B, S, D), jnp.float32), 'key': jax.random.normal(ks[1], (B, S, D), jnp.float32), 'value': jax.random.normal(ks[2], (B, S, D), jnp.float32), 'mask': jax.random.randint(ks[3], (B, 1, 1, S), 0, 2, jnp.int32), 'Wq': jax.random.normal(ks[4], (D, D), jnp.float32) / np.sqrt(D), 'bq': jnp.zeros((D,), jnp.float32), 'Wk': jax.random.normal(ks[5], (D, D), jnp.float32) / np.sqrt(D), 'bk': jnp.zeros((D,), jnp.float32), 'Wv': jax.random.normal(ks[6], (D, D), jnp.float32) / np.sqrt(D), 'bv': jnp.zeros((D,), jnp.float32), 'Wo': jax.random.normal(ks[7], (D, D), jnp.float32) / np.sqrt(D), 'bo': jnp.zeros((D,), jnp.float32)}
        return inp
    _L0_xattn_all = _L0_xattn_setup()
    _L0_xattn_in = {k: v for k, v in _L0_xattn_all.items() if k in ('Wq', 'bq', 'Wk', 'bk', 'Wv', 'bv', 'Wo', 'bo')}
    del _L0_xattn_all

    def _L0_ffn_setup():
        import jax, jax.numpy as jnp
        import numpy as np
        H = 256
        E = 8
        B, S = (4, 512)
        key = jax.random.key(seed)
        k1, k2, k3, k4 = jax.random.split(key, 4)
        x = jax.random.normal(k1, (B, S, H), dtype=jnp.float32)
        wg = jax.random.normal(k2, (H, E), dtype=jnp.float32) * 0.02
        W = jax.random.normal(k3, (E, H, H), dtype=jnp.float32) * 0.02
        b = jax.random.normal(k4, (E, H), dtype=jnp.float32) * 0.02
        return {'x': x, 'wg': wg, 'W': W, 'b': b}
    _L0_ffn_all = _L0_ffn_setup()
    _L0_ffn_in = {k: v for k, v in _L0_ffn_all.items() if k in ('wg', 'W', 'b')}
    del _L0_ffn_all
    return {'x': x, 'ctx_1024': ctx_1024, 'mask_Bx1x1xS2_ik0': mask_Bx1x1xS2_ik0, 'L0_xattn_Wq': _L0_xattn_in['Wq'], 'L0_xattn_bq': _L0_xattn_in['bq'], 'L0_xattn_Wk': _L0_xattn_in['Wk'], 'L0_xattn_bk': _L0_xattn_in['bk'], 'L0_xattn_Wv': _L0_xattn_in['Wv'], 'L0_xattn_bv': _L0_xattn_in['bv'], 'L0_xattn_Wo': _L0_xattn_in['Wo'], 'L0_xattn_bo': _L0_xattn_in['bo'], 'L0_ffn_wg': _L0_ffn_in['wg'], 'L0_ffn_W': _L0_ffn_in['W'], 'L0_ffn_b': _L0_ffn_in['b']}

def reference(x, ctx_1024, mask_Bx1x1xS2_ik0, L0_xattn_Wq, L0_xattn_bq, L0_xattn_Wk, L0_xattn_bk, L0_xattn_Wv, L0_xattn_bv, L0_xattn_Wo, L0_xattn_bo, L0_ffn_wg, L0_ffn_W, L0_ffn_b):
    import jax
    import jax.numpy as jnp

    def _L0_xattn_ref(query, key, value, mask, Wq, bq, Wk, bk, Wv, bv, Wo, bo):
        import jax, jax.numpy as jnp
        import numpy as np
        B, S, D, H = (2, 512, 256, 16)
        DEPTH = D // H

        def _split_heads(x):
            b, s, _ = x.shape
            return x.reshape(b, s, H, DEPTH).transpose(0, 2, 1, 3)
        q = _split_heads(query @ Wq + bq)
        k = _split_heads(key @ Wk + bk)
        v = _split_heads(value @ Wv + bv)
        scale = 1.0 / jnp.sqrt(jnp.asarray(DEPTH, jnp.float32))
        logits = jnp.einsum('bhqd,bhkd->bhqk', q, k) * scale
        logits = logits + mask.astype(jnp.float32) * -1000000000.0
        attn = jax.nn.softmax(logits, axis=-1)
        ctx = jnp.einsum('bhqk,bhkd->bhqd', attn, v)
        ctx = ctx.transpose(0, 2, 1, 3).reshape(query.shape[0], -1, D)
        return ctx @ Wo + bo

    def _L0_ffn_ref(x, wg, W, b):
        import jax, jax.numpy as jnp
        import numpy as np
        H = 256
        E = 8
        B, S = (4, 512)
        Bb, Ss, Hh = x.shape
        Ee = wg.shape[1]
        T = Bb * Ss
        C = T // Ee
        xt = x.reshape(T, Hh)
        logits = xt @ wg
        probs = jax.nn.softmax(logits, axis=-1)
        idx = jnp.argmax(probs, axis=-1)
        mask = jax.nn.one_hot(idx, Ee, dtype=xt.dtype)
        locations = jnp.cumsum(mask, axis=0) - mask
        mask = mask * (locations < C).astype(xt.dtype)
        gate = jnp.sum(probs * mask, axis=-1)
        loc_s = jnp.sum(locations * mask, axis=-1).astype(jnp.int32)
        loc_oh = jax.nn.one_hot(loc_s, C, dtype=xt.dtype)
        dispatch = mask[:, :, None] * loc_oh[:, None, :]
        combine = gate[:, None, None] * dispatch
        exp_in = jnp.einsum('tec,th->ech', dispatch, xt)
        exp_out = jnp.einsum('ech,efh->ecf', exp_in, W) + b[:, None, :]
        out = jnp.einsum('tec,ecf->tf', combine, exp_out)
        return out.reshape(Bb, Ss, Hh)
    x = x + _L0_xattn_ref(_layernorm(x, axis=-1), ctx_1024, ctx_1024, mask_Bx1x1xS2_ik0, L0_xattn_Wq, L0_xattn_bq, L0_xattn_Wk, L0_xattn_bk, L0_xattn_Wv, L0_xattn_bv, L0_xattn_Wo, L0_xattn_bo)
    x = x + _L0_ffn_ref(_layernorm(x, axis=-1), L0_ffn_wg, L0_ffn_W, L0_ffn_b)
    return x

_drawn_inputs = setup_inputs


def setup_inputs(seed=0):
    import zlib

    import numpy as np

    out = dict(_drawn_inputs(seed))
    spreads = {'L0_xattn_bq': (0.0, 0.351),
     'L0_xattn_bk': (0.0, 0.8),
     'L0_xattn_bv': (0.0, 0.1),
     'L0_xattn_bo': (0.0, 0.1)}
    factors = {'L0_ffn_b': 8.0}
    for name, (base, spread) in spreads.items():
        noise = np.random.default_rng([zlib.crc32(name.encode()), seed]).standard_normal(out[name].shape)
        drawn = base * np.exp(spread * noise) if base else spread * noise
        out[name] = jnp.asarray(drawn.astype(out[name].dtype))
    for name, factor in factors.items():
        out[name] = (out[name] * factor).astype(out[name].dtype)
    return out
```

```python
from contextlib import ExitStack

import concourse.bass as bass
from concourse import mybir

P = 128
ALU = mybir.AluOpType
ACT = mybir.ActivationFunctionType
AX = mybir.AxisListType
F32 = mybir.dt.float32
BF16 = mybir.dt.bfloat16
I32 = mybir.dt.int32
U32 = mybir.dt.uint32

RING = 3
EPS = 1e-5
NEG = -1e9
FAR = 1e6
PAIRS = [(0, 0), (0, 1), (1, 0), (0, 2), (2, 0), (1, 1)]


def xattn_moe(nc, x, ctx_in, mask, wq, bq, wk, bk, wv, bv, wo, bo, wg, w_exp, b_exp, out):
    B, S, D = x.shape
    E = wg.shape[1]
    T = B * S
    CAP = T // E
    H = 16
    DEP = D // H
    KC = D // P
    TC = S // P
    HH = H // 2
    QUADS = 2 * H // 4
    TERM = len(PAIRS) * DEP
    MROW = TERM
    XROW = TERM + 3
    KROWS = XROW + 3
    SCALE = float(DEP) ** -0.5
    ROW = D + 4
    MEAN, RSTD, GATE, TOK = D, D + 1, D + 2, D + 3
    GT = CAP // P
    assert S == 256 and D == 256 and KC == 2 and TC == 2 and KROWS <= P

    x_v = x.rearrange("b (c p) d -> b p c d", p=P)
    c_v = ctx_in.rearrange("b (c p) d -> b p c d", p=P)
    m_v = mask.rearrange("b o u (c p) -> b (o u p) c", p=P)
    out_v = out.rearrange("b (c p) d -> b p c d", p=P)
    out_rows = out.rearrange("b s d -> (b s) d")

    split_d = nc.dram_tensor("split_d", (RING, 2, 3, H * DEP, S), BF16, kind="Internal").ap()
    maskp_d = nc.dram_tensor("maskp_d", (B, 3, S), BF16, kind="Internal").ap()
    negmax_d = nc.dram_tensor("negmax_d", (RING, 6, H, S), BF16, kind="Internal").ap()
    slots_d = nc.dram_tensor("slots_d", (T, ROW), F32, kind="Internal").ap()

    with ExitStack() as es:
        def sb(name, shape, dt=F32):
            return es.enter_context(nc.sbuf_tensor(name, shape, dt))

        def sem(name):
            return es.enter_context(nc.semaphore(name))

        w_sb = {n: sb(f"w{n}", [P, KC, D]) for n in "qkvo"}
        wg_sb = sb("wg_sb", [P, KC, E])
        bias_qk = sb("bias_qk", [P, 2, KC])
        bv_sb = sb("bv_sb", [P, D])
        bo_sb = sb("bo_sb", [P, D])
        ident = sb("ident", [P, P])
        tri = sb("tri", [P, P], BF16)
        onesm = sb("onesm", [P, P], BF16)
        expo = sb("expo", [P, TC])
        iota8 = sb("iota8", [P, TC, E])
        far = sb("far", [P, 8 * ROW])
        ones_row = sb("ones_row", [3, H * S], BF16)
        zero_row = sb("zero_row", [3, H * S], BF16)
        mask_i = sb("mask_i", [B, S], I32)
        mask_f = sb("mask_f", [B, S])
        mask_p = sb("mask_p", [B, 3, S], BF16)
        x_sb = sb("x_sb", [P, RING, TC, D])
        c_sb = sb("c_sb", [P, RING, TC, D])
        st1 = sb("st1", [P, TC, 6])
        mv1 = sb("mv1", [P, TC, 2])
        rs1 = sb("rs1", [P, 2, TC])
        xn = sb("xn", [P, TC, D])
        xnT = sb("xnT", [P, KC, S])
        cT = sb("cT", [P, RING, KC, S])
        qk = sb("qk", [P, 2, KC, S])
        parts = sb("parts", [P, 2, 3, KC, S], BF16)
        qs = sb("qs", [P, RING, H, S], BF16)
        ks = sb("ks", [P, RING, H, S], BF16)
        v_sb = sb("v_sb", [P, RING, TC, H, 32])
        mx = sb("mx", [P, H, TC])
        nm = sb("nm", [HH, 2, S])
        nmp = sb("nmp", [HH, 2, 3, S], BF16)
        mask_c = sb("mask_c", [P, RING, TC], I32)
        mbias = sb("mbias", [P, RING, TC])
        probs = sb("probs", [P, 4, 2 * S])
        av = sb("av", [P, 2, 2, S])
        rec = sb("rec", [P, 2, TC, HH])
        an = sb("an", [P, TC, D])
        anT = sb("anT", [P, KC, S])
        xr = sb("xr", [P, RING, TC, D])
        rows = sb("rows", [P, RING, TC, ROW])
        st2 = sb("st2", [P, TC, 6])
        mv2 = sb("mv2", [P, TC, 2])
        rs2 = sb("rs2", [P, TC])
        x2n = sb("x2n", [P, TC, D])
        x2T = sb("x2T", [P, KC, S])
        lg = sb("lg", [P, TC, E])
        top = sb("top", [P, TC, 8])
        topi = sb("topi", [P, TC, 8], U32)
        expf = sb("expf", [P, TC])
        oh = sb("oh", [P, TC, E], BF16)
        seen = sb("seen", [P, TC + 1, E], BF16)
        ld = sb("ld", [P, TC, E])
        le = sb("le", [P, TC, E])
        lsum = sb("lsum", [P, TC])
        loc = sb("loc", [P, TC, E])
        locv = sb("locv", [P, TC])
        slotf = sb("slotf", [P, TC])
        late = sb("late", [P, TC])
        tokf = sb("tokf", [P, TC])
        sloti = sb("sloti", [P, RING, TC], U32)
        g_rows = sb("g_rows", [P, 2, GT, ROW])
        w_in = sb("w_in", [P, 2, KC, D])
        be_sb = sb("be_sb", [P, 2, D])
        weT = sb("weT", [P, 2, KC, D])
        g_n = sb("g_n", [P, GT, D])
        g_T = sb("g_T", [P, 2, KC, S])
        g_y = sb("g_y", [P, 2, D])
        g_out = sb("g_out", [P, 2, GT, D])
        g_tok = sb("g_tok", [P, 2, GT], U32)

        bank = [es.enter_context(nc.psum_tensor(f"bank{n}", [P, 512], F32)) for n in range(8)]
        P1, P2, CB, M = bank[0:2], bank[2:5], bank[5], bank[6:8]

        w_landed = sem("w_landed")
        mask_landed = sem("mask_landed")
        maskp_out = sem("maskp_out")
        const_out = sem("const_out")
        x_landed = [sem(f"x_landed{s}") for s in range(RING)]
        c_landed = [sem(f"c_landed{s}") for s in range(RING)]
        mc_landed = [sem(f"mc_landed{s}") for s in range(RING)]
        xr_landed = [sem(f"xr_landed{s}") for s in range(RING)]
        split_out = [sem(f"split_out{s}") for s in range(RING)]
        stack_landed = [sem(f"stack_landed{s}") for s in range(RING)]
        nm_out = [sem(f"nm_out{h}") for h in range(2)]
        nm_landed = [[sem(f"nm_landed{h}_{s}") for s in range(RING)] for h in range(2)]
        store_out = [sem(f"store_out{s}") for s in range(RING)]
        scat_out = [sem(f"scat_out{s}") for s in range(RING)]
        g_landed = [sem(f"g_landed{s}") for s in range(2)]
        we_landed = [sem(f"we_landed{s}") for s in range(2)]
        y_out = [sem(f"y_out{s}") for s in range(2)]
        pool_const = sem("pool_const")
        dve_const = sem("dve_const")
        TASKS = ["MTb", "CT", "C2T", "XT", "NT", "K", "O", "Q", "MTa", "V", "X2T", "C1T", "R", "L"]
        made = {t: sem(f"made_{t}") for t in TASKS}
        took = {t: sem(f"took_{t}") for t in TASKS}
        ln1_chain = sem("ln1_chain")
        rs1_chain = sem("rs1_chain")
        xn_ready = sem("xn_ready")
        split_chain = sem("split_chain")
        p1_ready = sem("p1_ready")
        max_done = sem("max_done")
        nm_chain = [sem("nm_chain0"), sem("nm_chain1")]
        p2_ready = sem("p2_ready")
        exp_done = sem("exp_done")
        pv_done = sem("pv_done")
        av_ready = [sem("av_ready0"), sem("av_ready1")]
        mbias_ready = sem("mbias_ready")
        rec_done = [sem("rec_done0"), sem("rec_done1")]
        xr_ready = sem("xr_ready")
        ln2_chain = sem("ln2_chain")
        rs2_chain = sem("rs2_chain")
        x2n_ready = sem("x2n_ready")
        route = sem("route")
        le_ready = sem("le_ready")
        rows_ready = sem("rows_ready")
        passed = sem("passed")
        we_T = sem("we_T")
        weT_ready = sem("weT_ready")
        gn_ready = sem("gn_ready")
        gT_made = sem("gT_made")
        gT_ready = sem("gT_ready")
        y_made = sem("y_made")
        y_chain = sem("y_chain")
        gtok_ready = sem("gtok_ready")

        ROUTE1, ROUTE2 = 11, 6
        ROUTE = ROUTE1 + ROUTE2
        STACK_DMAS = 2 * len(PAIRS) + 2
        STAGE = {"XT": 3, "CT": 3, "K": 3, "Q": 3, "V": 1, "MTa": 1, "MTb": 0, "C1T": 0,
                 "C2T": -1, "NT": -1, "O": -1, "X2T": -1, "R": -1, "L": -1}
        FULL = range(1, B - 3)
        assert len(FULL) % RING == 0

        def bank_of(task):
            return M[TASKS.index(task) % 2]

        def has(stage, i, known):
            return True if known is None else 0 <= known + stage < B

        def wait(eng, s, value):
            if isinstance(value, int) and value <= 0:
                return
            eng.wait_ge(s, value)

        def apart(eng):
            eng.sem_inc(passed, 1)

        def claim(pe, task, i, known):
            order = [t for t in TASKS if bank_of(t) is bank_of(task)]
            n = order.index(task)
            back = 0
            while True:
                n -= 1
                if n < 0:
                    n, back = len(order) - 1, back + 1
                if known is not None and known - back < -3:
                    return
                t = order[n]
                if has(STAGE[t], i, None if known is None else known - back):
                    wait(pe, took[t], i - back + STAGE[t] + 1)
                    return

        def slot_of(slot, stage):
            return (slot + stage) % RING

        block = es.enter_context(nc.Block())

        def looped(eng, turn):
            for i in range(-3, FULL[0]):
                turn(i, i, i % RING, lambda st, i=i: (i + st) // RING + 1)
            with eng.Fori(0, len(FULL) // RING) as j:
                for u in range(RING):
                    c = u + FULL[0]
                    turn(j * RING + c, None, c % RING, lambda st, c=c: j + ((c + st) // RING + 1))
            for i in range(FULL[-1] + 1, B + 1):
                turn(i, i, i % RING, lambda st, i=i: (i + st) // RING + 1)

        @block.sync
        def _(sp):
            for n, w in zip("qkvo", (wq, wk, wv, wo)):
                sp.dma_start(w_sb[n][:, :, :], w.rearrange("(c p) n -> p c n", p=P)).then_inc(w_landed, 16)
            sp.dma_start(wg_sb[:, :, :], wg.rearrange("(c p) e -> p c e", p=P)).then_inc(w_landed, 16)
            for n, v in enumerate((bq, bk)):
                sp.dma_start(bias_qk[:, n, :], v.rearrange("(c p) -> p c", p=P),
                             allow_slow_non_contiguous=True).then_inc(w_landed, 16)
            for t, v in ((bv_sb, bv), (bo_sb, bo)):
                sp.dma_start(t[:, :], v.rearrange("(o n) -> o n", o=1).to_broadcast([P, D])).then_inc(w_landed, 16)
            sp.dma_start(mask_i[:, :], mask.rearrange("b o u s -> (b o u) s")).then_inc(mask_landed, 16)
            sp.wait_ge(pool_const, 1)
            far_v = slots_d.rearrange("(n p r) c -> n p (r c)", p=P, r=8)
            for n in range(T // (8 * P)):
                sp.dma_start(far_v[n], far[:, :]).then_inc(const_out, 16)
            sp.wait_ge(dve_const, 2)
            for s in range(RING):
                sp.dma_start(negmax_d[s, 0:3].rearrange("r h t -> r (h t)"), zero_row[:, :]).then_inc(const_out, 16)
                sp.dma_start(ks[XROW:KROWS, s].rearrange("r h t -> r (h t)"), ones_row[:, :]).then_inc(const_out, 16)
            sp.wait_ge(dve_const, 7)
            sp.dma_start(maskp_d, mask_p[:, :, :]).then_inc(maskp_out, 16)
            sp.wait_ge(maskp_out, 16)

            def turn(i, known, slot, rnd):
                if has(3, i, known):
                    s = slot_of(slot, 3)
                    wait(sp, xn_ready, i + 1)
                    apart(sp)
                    sp.dma_start(x_sb[:, s], x_v[i + 3]).then_inc(x_landed[s], 16)
                    wait(sp, made["CT"], i + 1)
                    apart(sp)
                    sp.dma_start(c_sb[:, s], c_v[i + 3]).then_inc(c_landed[s], 16)
                if has(-1, i, known):
                    s = slot_of(slot, -1)
                    wait(sp, took["O"], i - 1)
                    apart(sp)
                    sp.dma_start(xr[:, s], x_v[i - 1]).then_inc(xr_landed[s], 16)
                if has(1, i, known):
                    s = slot_of(slot, 1)
                    wait(sp, mbias_ready, i - 1)
                    apart(sp)
                    sp.dma_start(mask_c[:, s], m_v[i + 1], allow_slow_non_contiguous=True).then_inc(mc_landed[s], 16)
                if has(2, i, known):
                    s = slot_of(slot, 2)
                    wait(sp, split_out[s], 16 * rnd(2))
                    apart(sp)
                    wait(sp, p2_ready, H * i)
                    apart(sp)
                    for side, stack in ((0, qs), (1, ks)):
                        src = split_d[s, side].rearrange("r (h d) t -> r d h t", d=DEP)
                        for n, pair in enumerate(PAIRS):
                            sp.dma_start(stack[n * DEP:(n + 1) * DEP, s], src[pair[side]]).then_inc(stack_landed[s], 16)
                    sp.dma_start(qs[MROW:MROW + 3, s].rearrange("r h t -> r (h t)"), ones_row[:, :]).then_inc(stack_landed[s], 16)
                    sp.dma_start(ks[MROW:MROW + 3, s], maskp_d[i + 2].rearrange("r (o t) -> r o t", o=1).to_broadcast([3, H, S])
                                 ).then_inc(stack_landed[s], 16)
                for half, stage in ((1, 0), (0, 1)):
                    if has(stage, i, known):
                        s = slot_of(slot, stage)
                        hs = slice(half * HH, (half + 1) * HH)
                        wait(sp, nm_chain[half], 4 * (i + stage + 1))
                        apart(sp)
                        sp.dma_start(negmax_d[s, 3:6, hs].rearrange("r h t -> h r t"), nmp[:, half]).then_inc(nm_out[half], 16)
                        wait(sp, nm_out[half], 16 * (i + stage + 1))
                        apart(sp)
                        sp.dma_start(qs[MROW:KROWS, s, hs].rearrange("r h t -> r (h t)"),
                                     negmax_d[s, :, hs].rearrange("r h t -> r (h t)")).then_inc(nm_landed[half][s], 16)
                if has(3, i, known):
                    s = slot_of(slot, 3)
                    wait(sp, split_chain, 4 * (i + 4))
                    apart(sp)
                    wait(sp, stack_landed[s], 16 * STACK_DMAS * (rnd(3) - 1) if known is None or rnd(3) > 1 else 0)
                    apart(sp)
                    sp.dma_start(split_d[s].rearrange("e r (c p) t -> p (e r c) t", p=P),
                                 parts[:, :, :, :, :].rearrange("p e r c t -> p (e r c) t")).then_inc(split_out[s], 16)
                if has(-1, i, known):
                    s = slot_of(slot, -1)
                    wait(sp, took["O"], i)
                    apart(sp)
                    sp.dma_start(out_v[i - 1], rows[:, s, :, 0:D]).then_inc(store_out[s], 16)

            looped(sp, turn)

            for s in range(RING):
                n = len(range(s, B, RING))
                sp.wait_ge(store_out[s], 16 * n)
                sp.wait_ge(scat_out[s], 32 * n)
            sp.wait_ge(const_out, 16 * (T // (8 * P) + 2 * RING))
            slots_v = slots_d.rearrange("(e g p) c -> e p g c", e=E, p=P)

            def load(e, s, waited):
                if waited:
                    wait(sp, y_chain, 4 * (e - 1))
                    apart(sp)
                    wait(sp, we_T, e - 1)
                    apart(sp)
                sp.dma_start(g_rows[:, s], slots_v[e]).then_inc(g_landed[s], 16)
                sp.dma_start(w_in[:, s], w_exp[e].rearrange("(c p) h -> p c h", p=P)).then_inc(we_landed[s], 16)
                sp.dma_start(be_sb[:, s], b_exp[e:e + 1, :].to_broadcast([P, D]) if isinstance(e, int) else
                             b_exp[bass.ds(e, 1), :].to_broadcast([P, D])).then_inc(we_landed[s], 16)

            for e in range(2):
                load(e, e, False)
            with sp.Fori(1, E // 2) as j:
                for s in range(2):
                    load(j * 2 + s, s, True)
            for s in range(2):
                sp.wait_ge(y_out[s], 16 * GT * (E // 2))

        @block.gpsimd
        def _(pool):
            g = nc.gpsimd
            g.memset(far[:, :], FAR).then_inc(pool_const, 1)
            g.memset(expo[:, :], -0.5).then_inc(pool_const, 1)
            g.memset(ident[:, :], 0.0).then_inc(pool_const, 1)
            g.memset(tri[:, :], 1.0).then_inc(pool_const, 1)
            pool.wait_ge(pool_const, 4)
            g.affine_select(out=ident[:, :], in_=ident[:, :], compare_op=ALU.not_equal, fill=1.0,
                            base=0, pattern=[[-1, P]], channel_multiplier=1).then_inc(pool_const, 1)
            g.affine_select(out=tri[:, :], in_=tri[:, :], compare_op=ALU.is_gt, fill=0.0,
                            base=0, pattern=[[1, P]], channel_multiplier=-1).then_inc(pool_const, 1)
            g.iota(iota8[:, :, :], pattern=[[0, TC], [1, E]], base=0, channel_multiplier=0,
                   allow_small_or_imprecise_dtypes=True).then_inc(pool_const, 1)
            g.iota(tokf[:, :], pattern=[[P, TC]], base=-S, channel_multiplier=1,
                   allow_small_or_imprecise_dtypes=True).then_inc(pool_const, 1)

            def negmax_parts(half, b):
                c = nm_chain[half]
                pool.wait_ge(took["MTb" if half else "MTa"], b + 1)
                wait(pool, nm_out[half], 16 * b)
                apart(pool)
                g.tensor_copy(nmp[:, half, 0], nm[:, half]).then_inc(c, 1)
                pool.wait_ge(c, 4 * b + 1)
                apart(pool)
                g.tensor_tensor(nm[:, half], nm[:, half], nmp[:, half, 0], ALU.subtract).then_inc(c, 1)
                pool.wait_ge(c, 4 * b + 2)
                apart(pool)
                g.tensor_copy(nmp[:, half, 1], nm[:, half]).then_inc(c, 1)
                pool.wait_ge(c, 4 * b + 3)
                apart(pool)
                g.tensor_tensor(nmp[:, half, 2], nm[:, half], nmp[:, half, 1], ALU.subtract).then_inc(c, 1)

            def turn(i, known, slot, rnd):
                s3 = slot_of(slot, 3)
                if has(3, i, known):
                    pool.wait_ge(ln1_chain, 4 * (i + 4))
                    apart(pool)
                    g.tensor_scalar(rs1[:, 0], mv1[:, :, 1], EPS, None, ALU.add).then_inc(rs1_chain, 1)
                    pool.wait_ge(rs1_chain, 2 * (i + 3) + 1)
                    apart(pool)
                    g.tensor_tensor(rs1[:, 1], rs1[:, 0], expo[:, :], ALU.pow).then_inc(rs1_chain, 1)
                if has(0, i, known):
                    negmax_parts(1, i)
                if has(-1, i, known):
                    s = slot_of(slot, -1)
                    if known is not None and known == 1 or known is None:
                        pass
                    pool.wait_ge(w_landed, 16 * 9)
                    pool.wait_ge(xr_landed[s], 16 * rnd(-1))
                    apart(pool)
                    g.tensor_tensor(xr[:, s], xr[:, s], bo_sb[:, :].rearrange("p (o n) -> p o n", o=1).to_broadcast([P, TC, D]),
                                    ALU.add).then_inc(xr_ready, 1)
                    pool.wait_ge(ln2_chain, 4 * i)
                    apart(pool)
                    g.tensor_scalar(rs2[:, :], mv2[:, :, 1], EPS, None, ALU.add).then_inc(rs2_chain, 1)
                    pool.wait_ge(rs2_chain, 3 * (i - 1) + 1)
                    apart(pool)
                    g.tensor_tensor(rows[:, s, :, RSTD], rs2[:, :], expo[:, :], ALU.pow).then_inc(rs2_chain, 1)
                    g.tensor_copy(rows[:, s, :, MEAN], mv2[:, :, 0]).then_inc(rs2_chain, 1)
                if has(3, i, known):
                    pool.wait_ge(took["K"], i + 4)
                    pool.wait_ge(took["Q"], i + 4)
                    wait(pool, split_out[slot_of(slot, 2)], 16 * rnd(2) if known is None or known + 2 >= 0 else 0)
                    apart(pool)
                    g.tensor_copy(parts[:, :, 0], qk[:, :, :, :]).then_inc(split_chain, 1)
                    pool.wait_ge(split_chain, 4 * (i + 3) + 1)
                    apart(pool)
                    g.tensor_tensor(qk[:, :, :, :], qk[:, :, :, :], parts[:, :, 0], ALU.subtract).then_inc(split_chain, 1)
                if has(1, i, known):
                    negmax_parts(0, i + 1)
                if has(3, i, known):
                    pool.wait_ge(split_chain, 4 * (i + 3) + 2)
                    apart(pool)
                    g.tensor_copy(parts[:, :, 1], qk[:, :, :, :]).then_inc(split_chain, 1)
                    pool.wait_ge(split_chain, 4 * (i + 3) + 3)
                    apart(pool)
                    g.tensor_tensor(parts[:, :, 2], qk[:, :, :, :], parts[:, :, 1], ALU.subtract).then_inc(split_chain, 1)
                if has(-1, i, known):
                    s = slot_of(slot, -1)
                    if known is not None:
                        pool.wait_ge(const_out, 16 * (T // (8 * P) + 2 * RING))
                    pool.wait_ge(rows_ready, i)
                    apart(pool)
                    for t in range(TC):
                        g.indirect_dma_start(slots_d, bass.IndirectOffsetOnAxis(ap=sloti[:, s, t:t + 1], axis=0),
                                             rows[:, s, t, :], None, bounds_check=T - 1, oob_is_err=False
                                             ).then_inc(scat_out[s], 16)

            looped(pool, turn)

            def finish(e, s):
                pool.wait_ge(y_chain, 4 * (e + 1))
                pool.wait_ge(gtok_ready, e + 1)
                apart(pool)
                for t in range(GT):
                    g.indirect_dma_start(out_rows, bass.IndirectOffsetOnAxis(ap=g_tok[:, s, t:t + 1], axis=0),
                                         g_out[:, s, t, :], None, bounds_check=T - 1, oob_is_err=False
                                         ).then_inc(y_out[s], 16)

            with pool.Fori(0, E // 2) as j:
                for s in range(2):
                    finish(j * 2 + s, s)

        @block.scalar
        def _(act):
            a = nc.scalar

            def evac(task, b, dst):
                act.wait_ge(made[task], b + 1)
                a.activation(dst, bank_of(task)[:, :], ACT.Copy).then_inc(took[task], 1)

            def qk_evac(task, side, b):
                act.wait_ge(made[task], b + 1)
                wait(act, split_chain, 4 * b)
                for c in range(KC):
                    r = a.activation(qk[:, side, c], bank_of(task)[:, c * S:(c + 1) * S], ACT.Identity,
                                     bias=bias_qk[:, side, c:c + 1])
                r.then_inc(took[task], 1)

            def neg_evac(task, half, b):
                act.wait_ge(made[task], b + 1)
                wait(act, nm_chain[half], 4 * b)
                a.activation(nm[:, half], bank_of(task)[0:HH, 0:S], ACT.Copy, scale=-1.0).then_inc(took[task], 1)

            def sums_evac(half, b, quads):
                act.wait_ge(pv_done, quads)
                wait(act, made["C2T" if half else "C1T"], b)
                a.activation(av[:, half], CB[:, :].rearrange("p (g t) -> p g t", g=2), ACT.Copy).then_inc(av_ready[half], 1)

            def turn(i, known, slot, rnd):
                for k in range(QUADS):
                    if has(0, i, known):
                        if k == 0:
                            act.wait_ge(mbias_ready, i + 1)
                        c = k % 2
                        for n in (2 * k, 2 * k + 1):
                            act.wait_ge(p2_ready, H * i + (n + 1))
                            wait(act, pv_done, QUADS * i + (n // 2 - 1))
                            a.activation(probs[:, n % 4], P2[(slot * H + n) % 3][:, :], ACT.Exp,
                                         bias=mbias[:, slot, c:c + 1], scale=SCALE).then_inc(exp_done, 1)
                    if k == 0 and has(-1, i, known):
                        sums_evac(1, i - 1, QUADS * i)
                    if k == 0 and has(0, i, known):
                        neg_evac("MTb", 1, i)
                    if k == 1 and has(3, i, known):
                        wait(act, made["V"], i + 1)
                        evac("CT", i + 3, cT[:, slot_of(slot, 3)].rearrange("p c t -> p (c t)"))
                    if k == 2 and has(3, i, known):
                        evac("XT", i + 3, xnT[:, :, :].rearrange("p c t -> p (c t)"))
                    if k == 2 and has(-1, i, known):
                        evac("NT", i - 1, anT[:, :, :].rearrange("p c t -> p (c t)"))
                    if k == 3 and has(3, i, known):
                        if known is not None:
                            act.wait_ge(w_landed, 16 * 9)
                        qk_evac("K", 1, i + 3)
                    if k == 4 and has(3, i, known):
                        qk_evac("Q", 0, i + 3)
                    if k == 4 and has(1, i, known):
                        neg_evac("MTa", 0, i + 1)
                    if k == 4 and has(0, i, known):
                        sums_evac(0, i, QUADS * i + QUADS // 2)
                    if k == 5 and has(-1, i, known):
                        evac("X2T", i - 1, x2T[:, :, :].rearrange("p c t -> p (c t)"))
                    if k == 7 and has(-1, i, known):
                        act.wait_ge(route, ROUTE * (i - 1) + ROUTE1)
                        a.activation(le[:, :, :], ld[:, :, :], ACT.Exp).then_inc(le_ready, 1)

            looped(act, turn)

            def expert(e, s):
                act.wait_ge(we_T, e + 1)
                a.activation(weT[:, s].rearrange("p c f -> p (c f)"), M[s][:, :], ACT.Copy).then_inc(weT_ready, 1)
                for r in range(2):
                    act.wait_ge(gT_made, 2 * e + r + 1)
                    a.activation(g_T[:, r].rearrange("p c t -> p (c t)"), P1[r][:, :], ACT.Copy).then_inc(gT_ready, 1)

            with act.Fori(0, E // 2) as j:
                for s in range(2):
                    expert(j * 2 + s, s)

        @block.vector
        def _(dve):
            v = nc.vector
            v.memset(ones_row[:, :], 1.0).then_inc(dve_const, 1)
            v.memset(zero_row[:, :], 0.0).then_inc(dve_const, 1)
            v.memset(onesm[:, :], 1.0)
            v.memset(seen[:, :, :], 0.0)
            for s in range(RING):
                v.memset(v_sb[:, s], 1.0)
            dve.wait_ge(mask_landed, 16)
            v.tensor_scalar(mask_f[:, :], mask_i[:, :], NEG / SCALE, None, ALU.mult).then_inc(dve_const, 1)
            dve.wait_ge(dve_const, 3)
            v.tensor_copy(mask_p[:, 0], mask_f[:, :]).then_inc(dve_const, 1)
            dve.wait_ge(dve_const, 4)
            v.tensor_tensor(mask_f[:, :], mask_f[:, :], mask_p[:, 0], ALU.subtract).then_inc(dve_const, 1)
            dve.wait_ge(dve_const, 5)
            v.tensor_copy(mask_p[:, 1], mask_f[:, :]).then_inc(dve_const, 1)
            dve.wait_ge(dve_const, 6)
            v.tensor_tensor(mask_p[:, 2], mask_f[:, :], mask_p[:, 1], ALU.subtract).then_inc(dve_const, 1)
            dve.wait_ge(pool_const, 8)

            def normalise(task, half, b):
                src = bank_of(task)[:, :].rearrange("p (q h e) -> p q h e", q=TC, e=32)
                dve.wait_ge(made[task], b + 1)
                v.reciprocal(rec[:, half], src[:, :, :, DEP]).then_inc(rec_done[half], 1)
                dve.wait_ge(rec_done[half], b + 1)
                wait(dve, made["NT"], b)
                v.tensor_tensor(an[:, :, half * P:(half + 1) * P].rearrange("p q (h d) -> p q h d", d=DEP),
                                src[:, :, :, 0:DEP],
                                rec[:, half].rearrange("p q (h o) -> p q h o", o=1).to_broadcast([P, TC, HH, DEP]),
                                ALU.mult).then_inc(took[task], 1)

            def statistics(src, st, mv, chain, b):
                for t in range(TC):
                    v.bn_stats(st[:, t], src[:, t]).then_inc(chain, 1)
                for t in range(TC):
                    dve.wait_ge(chain, 4 * b + t + 1)
                    apart(dve)
                    v.bn_aggr(mv[:, t], st[:, t]).then_inc(chain, 1)

            def turn(i, known, slot, rnd):
                sp1 = slot_of(slot, -1)
                for k in range(QUADS):
                    if has(1, i, known):
                        for h in (2 * k, 2 * k + 1):
                            dve.wait_ge(p1_ready, H * (i + 1) + (h + 1))
                            if h == 0:
                                wait(dve, made["MTa"], i + 1)
                            if h == HH:
                                wait(dve, made["MTb"], i + 1)
                            v.tensor_reduce(mx[:, h], P1[h % 2][:, :].rearrange("p (q t) -> p q t", q=TC),
                                            AX.X, ALU.max).then_inc(max_done, 1)
                    if k == 0 and has(3, i, known):
                        dve.wait_ge(x_landed[slot_of(slot, 3)], 16 * rnd(3))
                        wait(dve, rs1_chain, 2 * (i + 3))
                        wait(dve, xn_ready, i + 3)
                        statistics(x_sb[:, slot_of(slot, 3)], st1, mv1, ln1_chain, i + 3)
                    if k == 0 and has(1, i, known):
                        s = slot_of(slot, 1)
                        dve.wait_ge(mc_landed[s], 16 * rnd(1))
                        wait(dve, exp_done, H * (i - 1))
                        v.tensor_scalar(mbias[:, s], mask_c[:, s], NEG, None, ALU.mult).then_inc(mbias_ready, 1)
                    if k == 1 and has(-1, i, known):
                        normalise("C2T", 1, i - 1)
                    if k == 1 and has(3, i, known):
                        dve.wait_ge(rs1_chain, 2 * (i + 4))
                        wait(dve, made["XT"], i + 3)
                        for t in range(TC):
                            r = v.tensor_scalar(xn[:, t], x_sb[:, slot_of(slot, 3), t], mv1[:, t, 0:1],
                                                rs1[:, 1, t:t + 1], ALU.subtract, ALU.mult)
                        r.then_inc(xn_ready, 1)
                    if k == 3 and has(-1, i, known):
                        dve.wait_ge(made["O"], i)
                        dve.wait_ge(xr_ready, i)
                        if known is None or known >= 4:
                            dve.wait_ge(store_out[sp1], 16 * (rnd(-1) - 1))
                            dve.wait_ge(scat_out[sp1], 32 * (rnd(-1) - 1))
                        v.tensor_tensor(rows[:, sp1, :, 0:D], bank_of("O")[:, :].rearrange("p (q n) -> p q n", q=TC),
                                        xr[:, sp1], ALU.add).then_inc(took["O"], 1)
                        dve.wait_ge(took["O"], i)
                        wait(dve, rs2_chain, 3 * (i - 1))
                        statistics(rows[:, sp1, :, 0:D], st2, mv2, ln2_chain, i - 1)
                    if k == 4 and has(-1, i, known):
                        dve.wait_ge(rs2_chain, 3 * i)
                        wait(dve, made["X2T"], i - 1)
                        for t in range(TC):
                            r = v.tensor_scalar(x2n[:, t], rows[:, sp1, t, 0:D], rows[:, sp1, t, MEAN:MEAN + 1],
                                                rows[:, sp1, t, RSTD:RSTD + 1], ALU.subtract, ALU.mult)
                        r.then_inc(x2n_ready, 1)
                    if k == 5 and has(1, i, known):
                        s = slot_of(slot, 1)
                        dve.wait_ge(made["V"], i + 2)
                        if known is not None:
                            dve.wait_ge(w_landed, 16 * 9)
                        wait(dve, pv_done, QUADS * (i - 1))
                        v.tensor_tensor(v_sb[:, s, :, :, 0:DEP],
                                        bank_of("V")[:, :].rearrange("p (c h d) -> p c h d", c=TC, d=DEP),
                                        bv_sb[:, :].rearrange("p (o h d) -> p o h d", o=1, d=DEP).to_broadcast([P, TC, H, DEP]),
                                        ALU.add).then_inc(took["V"], 1)
                    if k == 5 and has(0, i, known):
                        normalise("C1T", 0, i)
                    if k == 6 and has(-1, i, known):
                        b = i - 1
                        n = [0]

                        def step(ins):
                            n[0] += 1
                            ins.then_inc(route, 1)

                        def steps_done():
                            dve.wait_ge(route, ROUTE * b + n[0])

                        dve.wait_ge(made["R"], i)
                        v.tensor_copy(lg[:, :, :], bank_of("R")[:, 0:TC * E].rearrange("p (q e) -> p q e", e=E)
                                      ).then_inc(took["R"], 1)
                        dve.wait_ge(took["R"], i)
                        apart(dve)
                        for t in range(TC):
                            step(v.max(top[:, t], lg[:, t]))
                        wait(dve, made["L"], i - 1)
                        step(v.tensor_copy(seen[:, 0], seen[:, TC]))
                        steps_done()
                        apart(dve)
                        for t in range(TC):
                            step(v.max_index(topi[:, t], top[:, t], lg[:, t]))
                        step(v.tensor_tensor(ld[:, :, :], lg[:, :, :], top[:, :, 0:1].to_broadcast([P, TC, E]), ALU.subtract))
                        steps_done()
                        step(v.tensor_copy(expf[:, :], topi[:, :, 0]))
                        steps_done()
                        step(v.tensor_tensor(oh[:, :, :], iota8[:, :, :],
                                             expf[:, :].rearrange("p (q o) -> p q o", o=1).to_broadcast([P, TC, E]), ALU.is_equal))
                        for t in range(TC):
                            steps_done()
                            step(v.tensor_tensor(seen[:, t + 1], seen[:, t], oh[:, t], ALU.add))
                        step(v.tensor_scalar(tokf[:, :], tokf[:, :], float(S), None, ALU.add))
                        assert n[0] == ROUTE1
                    if k == 7 and has(-1, i, known):
                        b = i - 1
                        n = [ROUTE1]

                        def step(ins):
                            n[0] += 1
                            ins.then_inc(route, 1)

                        def steps_done():
                            dve.wait_ge(route, ROUTE * b + n[0])

                        steps_done()
                        v.tensor_copy(rows[:, sp1, :, TOK], tokf[:, :])
                        dve.wait_ge(made["L"], i)
                        v.tensor_tensor(loc[:, :, :], bank_of("L")[:, 0:TC * E].rearrange("p (q e) -> p q e", e=E),
                                        oh[:, :, :], ALU.mult).then_inc(took["L"], 1)
                        dve.wait_ge(took["L"], i)
                        step(v.tensor_reduce(locv[:, :], loc[:, :, :], AX.X, ALU.add))
                        dve.wait_ge(le_ready, i)
                        step(v.tensor_reduce(lsum[:, :], le[:, :, :], AX.X, ALU.add))
                        steps_done()
                        step(v.tensor_scalar(late[:, :], locv[:, :], float(CAP), FAR, ALU.is_ge, ALU.mult))
                        step(v.scalar_tensor_tensor(out=slotf[:, :], in0=expf[:, :], scalar=float(CAP), in1=locv[:, :],
                                                    op0=ALU.mult, op1=ALU.add))
                        step(v.reciprocal(rows[:, sp1, :, GATE], lsum[:, :]))
                        steps_done()
                        step(v.tensor_tensor(slotf[:, :], slotf[:, :], late[:, :], ALU.add))
                        steps_done()
                        v.tensor_copy(sloti[:, sp1], slotf[:, :]).then_inc(rows_ready, 1)
                        assert n[0] == ROUTE

            looped(dve, turn)

            def finish(e, s, j):
                if not isinstance(j, int) or j > 0:
                    dve.wait_ge(y_out[s], 16 * GT * j)
                v.tensor_copy(g_tok[:, s], g_rows[:, s, :, TOK]).then_inc(gtok_ready, 1)
                dve.wait_ge(we_landed[s], 32 * (j + 1))
                for r in range(2):
                    dve.wait_ge(y_made, 2 * e + r + 1)
                    v.tensor_tensor(g_y[:, :, :], P2[r][:, :].rearrange("p (q n) -> p q n", q=2),
                                    be_sb[:, s].rearrange("p (o n) -> p o n", o=1).to_broadcast([P, 2, D]),
                                    ALU.add).then_inc(y_chain, 1)
                    dve.wait_ge(y_chain, 4 * e + 2 * r + 1)
                    for q in range(2):
                        t = 2 * r + q
                        o = v.scalar_tensor_tensor(out=g_out[:, s, t], in0=g_y[:, q], scalar=g_rows[:, s, t, GATE:GATE + 1],
                                                   in1=g_rows[:, s, t, 0:D], op0=ALU.mult, op1=ALU.add)
                    o.then_inc(y_chain, 1)
                    if r == 0:
                        dve.wait_ge(y_chain, 4 * e + 2)

            def pair(j):
                for s in range(2):
                    e = j * 2 + s
                    dve.wait_ge(g_landed[s], 16 * (j + 1))
                    wait(dve, gT_made, 2 * e)
                    if not isinstance(e, int) or e > 0:
                        dve.wait_ge(y_chain, 4 * e)
                    for t in range(GT):
                        r = v.tensor_scalar(g_n[:, t], g_rows[:, s, t, 0:D], g_rows[:, s, t, MEAN:MEAN + 1],
                                            g_rows[:, s, t, RSTD:RSTD + 1], ALU.subtract, ALU.mult)
                    r.then_inc(gn_ready, 1)
                    finish(e, s, j)

            pair(0)
            with dve.Fori(1, E // 2) as j:
                pair(j)

        @block.tensor
        def _(pe):
            t_ = nc.tensor
            pe.wait_ge(pool_const, 8)
            pe.wait_ge(dve_const, 7)

            def transposes(task, src, ready):
                o = bank_of(task)
                for c in range(2):
                    for t in range(2):
                        r = t_.transpose(o[:, c * S + t * P:c * S + (t + 1) * P], src(c, t), ident[:, :])
                r.then_inc(made[task], 1)

            def product(task, lhs, rhs):
                o = bank_of(task)
                for n in range(2):
                    for c in range(2):
                        r = t_.matmul(o[:, n * S:(n + 1) * S], lhs(c, n), rhs(c, n), start=(c == 0), stop=(c == 1))
                r.then_inc(made[task], 1)

            def times_v(i, known, k, slot):
                g, c = k // 2, k % 2
                pe.wait_ge(exp_done, H * i + (2 * k + 2))
                if k == 0:
                    pe.wait_ge(took["V"], i + 1)
                    wait(pe, av_ready[1], i)
                if k == QUADS // 2:
                    pe.wait_ge(av_ready[0], i + 1)
                for j in range(4):
                    n = 2 * k + j // 2
                    r = t_.matmul(CB[32 * j:32 * j + 32, (g % 2) * S:(g % 2 + 1) * S], v_sb[:, slot, c, 4 * g + j, :],
                                  probs[:, n % 4, (j % 2) * S:(j % 2 + 1) * S], start=(c == 0), stop=(c == 1))
                r.then_inc(pv_done, 1)

            def negmax(task, half, b, i, known):
                pe.wait_ge(max_done, H * b + HH * (half + 1))
                claim(pe, task, i, known)
                for q in range(TC):
                    r = t_.transpose(bank_of(task)[0:HH, q * P:(q + 1) * P], mx[:, half * HH:(half + 1) * HH, q], ident[:, :])
                r.then_inc(made[task], 1)

            def turn(i, known, slot, rnd):
                if known is not None and known == -3:
                    pe.wait_ge(w_landed, 16 * 9)
                if known is not None and known == -1:
                    pe.wait_ge(const_out, 16 * (T // (8 * P) + 2 * RING))
                for k in range(QUADS):
                    g, c = k // 2, k % 2
                    if has(0, i, known):
                        if k == 0:
                            pe.wait_ge(nm_landed[0][slot], 16 * rnd(0))
                        if k == QUADS // 2:
                            pe.wait_ge(nm_landed[1][slot], 16 * rnd(0))
                        for n in (2 * k, 2 * k + 1):
                            wait(pe, exp_done, H * i + (n - 2))
                            for j in range(2):
                                h = 4 * g + 2 * (n % 2) + j
                                r = t_.matmul(P2[(slot * H + n) % 3][:, j * S:(j + 1) * S],
                                              ks[0:KROWS, slot, h, c * P:(c + 1) * P], qs[0:KROWS, slot, h, :],
                                              start=True, stop=True)
                            r.then_inc(p2_ready, 1)
                    if has(1, i, known):
                        s = slot_of(slot, 1)
                        if k == 0:
                            pe.wait_ge(stack_landed[s], 16 * STACK_DMAS * rnd(1))
                        for h in (2 * k, 2 * k + 1):
                            wait(pe, max_done, H * (i + 1) + (h - 1))
                            for q in range(TC):
                                r = t_.matmul(P1[h % 2][:, q * S:(q + 1) * S], qs[0:XROW, s, h, q * P:(q + 1) * P],
                                              ks[0:XROW, s, h, :], start=True, stop=True)
                            r.then_inc(p1_ready, 1)
                    if k > 0 and has(0, i, known):
                        times_v(i, known, k - 1, slot)
                    if k == 0 and has(-1, i, known):
                        times_v(i - 1, known, QUADS - 1, slot_of(slot, -1))
                    if k == 0 and has(0, i, known):
                        negmax("MTb", 1, i, i, known)
                    if k == 1 and has(3, i, known):
                        s = slot_of(slot, 3)
                        pe.wait_ge(c_landed[s], 16 * rnd(3))
                        claim(pe, "CT", i, known)
                        transposes("CT", lambda cc, t: c_sb[:, s, t, cc * P:(cc + 1) * P], None)
                    if k == 1 and has(-1, i, known):
                        pe.wait_ge(av_ready[1], i)
                        claim(pe, "C2T", i, known)
                        transposes("C2T", lambda q, gg: av[:, 1, gg, q * P:(q + 1) * P], None)
                    if k == 2 and has(3, i, known):
                        pe.wait_ge(xn_ready, i + 4)
                        claim(pe, "XT", i, known)
                        transposes("XT", lambda cc, t: xn[:, t, cc * P:(cc + 1) * P], None)
                    if k == 2 and has(-1, i, known):
                        pe.wait_ge(took["C2T"], i)
                        claim(pe, "NT", i, known)
                        transposes("NT", lambda cc, t: an[:, t, cc * P:(cc + 1) * P], None)
                    if k == 3 and has(3, i, known):
                        s = slot_of(slot, 3)
                        pe.wait_ge(took["CT"], i + 4)
                        claim(pe, "K", i, known)
                        product("K", lambda cc, n: w_sb["k"][:, cc, n * P:(n + 1) * P], lambda cc, n: cT[:, s, cc, :])
                    if k == 3 and has(-1, i, known):
                        pe.wait_ge(took["NT"], i)
                        claim(pe, "O", i, known)
                        product("O", lambda cc, n: anT[:, cc, n * P:(n + 1) * P], lambda cc, n: w_sb["o"][:, cc, :])
                    if k == 4 and has(3, i, known):
                        pe.wait_ge(took["XT"], i + 4)
                        claim(pe, "Q", i, known)
                        product("Q", lambda cc, n: w_sb["q"][:, cc, n * P:(n + 1) * P], lambda cc, n: xnT[:, cc, :])
                    if k == 4 and has(1, i, known):
                        negmax("MTa", 0, i + 1, i, known)
                    if k == 5 and has(1, i, known):
                        s1 = slot_of(slot, 1)
                        claim(pe, "V", i, known)
                        product("V", lambda cc, n: cT[:, s1, cc, n * P:(n + 1) * P], lambda cc, n: w_sb["v"][:, cc, :])
                    if k == 5 and has(-1, i, known):
                        pe.wait_ge(x2n_ready, i)
                        claim(pe, "X2T", i, known)
                        transposes("X2T", lambda cc, t: x2n[:, t, cc * P:(cc + 1) * P], None)
                    if k == 5 and has(0, i, known):
                        pe.wait_ge(av_ready[0], i + 1)
                        claim(pe, "C1T", i, known)
                        transposes("C1T", lambda q, gg: av[:, 0, gg, q * P:(q + 1) * P], None)
                    if k == 6 and has(-1, i, known):
                        pe.wait_ge(took["X2T"], i)
                        claim(pe, "R", i, known)
                        for t in range(TC):
                            for cc in range(KC):
                                r = t_.matmul(bank_of("R")[:, t * E:(t + 1) * E], x2T[:, cc, t * P:(t + 1) * P], wg_sb[:, cc, :],
                                              start=(cc == 0), stop=(cc == KC - 1))
                        r.then_inc(made["R"], 1)
                    if k == 7 and has(-1, i, known):
                        pe.wait_ge(route, ROUTE * (i - 1) + ROUTE1)
                        claim(pe, "L", i, known)
                        o = bank_of("L")[:, 0:TC * E]
                        t_.matmul(o, tri[:, :], oh[:, :, :].rearrange("p q e -> p (q e)"), start=True, stop=False)
                        t_.matmul(o, onesm[:, :], seen[:, 0:TC, :].rearrange("p q e -> p (q e)"), start=False, stop=True
                                  ).then_inc(made["L"], 1)

            looped(pe, turn)

            def expert(e, s, j):
                pe.wait_ge(we_landed[s], 32 * (j + 1))
                if isinstance(e, int):
                    pe.wait_ge(took["L"], B)
                    pe.wait_ge(took["R"], B)
                if not isinstance(e, int) or e >= 2:
                    pe.wait_ge(weT_ready, e - 1)
                    pe.wait_ge(y_made, 2 * (e - 1))
                for c in range(KC):
                    for f in range(KC):
                        r = t_.transpose(M[s][:, c * D + f * P:c * D + (f + 1) * P], w_in[:, s, f, c * P:(c + 1) * P], ident[:, :])
                r.then_inc(we_T, 1)
                pe.wait_ge(gn_ready, e + 1)
                for r2 in range(2):
                    if not isinstance(e, int) or e > 0:
                        pe.wait_ge(gT_ready, 2 * e + (r2 - 1))
                    for c in range(KC):
                        for q in range(2):
                            r = t_.transpose(P1[r2][:, c * S + q * P:c * S + (q + 1) * P],
                                             g_n[:, 2 * r2 + q, c * P:(c + 1) * P], ident[:, :])
                    r.then_inc(gT_made, 1)
                pe.wait_ge(weT_ready, e + 1)
                for r2 in range(2):
                    pe.wait_ge(gT_ready, 2 * e + (r2 + 1))
                    if not isinstance(e, int) or e > 0:
                        pe.wait_ge(y_chain, 4 * e + (2 * r2 - 3))
                    for q in range(2):
                        for c in range(KC):
                            r = t_.matmul(P2[r2][:, q * D:(q + 1) * D], g_T[:, r2, c, q * P:(q + 1) * P], weT[:, s, c, :],
                                          start=(c == 0), stop=(c == KC - 1))
                    r.then_inc(y_made, 1)

            for s in range(2):
                expert(s, s, 0)
            with pe.Fori(1, E // 2) as j:
                for s in range(2):
                    expert(j * 2 + s, s, j)


_INS = ["x", "ctx_1024", "mask_Bx1x1xS2_ik0", "L0_xattn_Wq", "L0_xattn_bq", "L0_xattn_Wk", "L0_xattn_bk",
        "L0_xattn_Wv", "L0_xattn_bv", "L0_xattn_Wo", "L0_xattn_bo", "L0_ffn_wg", "L0_ffn_W", "L0_ffn_b"]


def kernel(**inputs):
    import numpy as _np
    import concourse.bacc as _bacc
    from concourse import mybir as _mybir
    from concourse.bass_utils import run_bass_kernel_spmd as _run

    nc = _bacc.Bacc("TRN2", target_bir_lowering=False, num_devices=1)
    arrays, args = {}, []
    for name in _INS:
        a = _np.ascontiguousarray(inputs[name])
        arrays[f"in_{name}"] = a
        args.append(nc.dram_tensor(f"in_{name}", a.shape, _mybir.dt.from_np(a.dtype), kind="ExternalInput").ap())
    shape = inputs["x"].shape
    out = nc.dram_tensor("out_0", shape, _mybir.dt.float32, kind="ExternalOutput").ap()
    xattn_moe(nc, *args, out)
    r = _run(nc, [arrays], core_ids=[0])
    return r.results[0]["out_0"]
```

```python
from contextlib import ExitStack

import concourse.bass as bass
from concourse import mybir

P = 128
ALU = mybir.AluOpType
ACT = mybir.ActivationFunctionType
AX = mybir.AxisListType
F32 = mybir.dt.float32
BF16 = mybir.dt.bfloat16
I32 = mybir.dt.int32
U32 = mybir.dt.uint32

RING = 3
EPS = 1e-5
NEG = -1e9
FAR = 1e6
PAIRS = [(0, 0), (0, 1), (1, 0), (0, 2), (2, 0), (1, 1)]


def xattn_moe(nc, x, ctx_in, mask, wq, bq, wk, bk, wv, bv, wo, bo, wg, w_exp, b_exp, out):
    B, S, D = x.shape
    E = wg.shape[1]
    T = B * S
    CAP = T // E
    H = 16
    DEP = D // H
    KC = D // P
    TC = S // P
    HH = H // 2
    QUADS = 2 * H // 4
    TERM = len(PAIRS) * DEP
    MROW = TERM
    XROW = TERM + 3
    KROWS = XROW + 3
    SCALE = float(DEP) ** -0.5
    ROW = D + 4
    MEAN, RSTD, GATE, TOK = D, D + 1, D + 2, D + 3
    GT = CAP // P
    FARR = 4
    FARS = T // (FARR * P)
    GR = 6
    assert S == 256 and D == 256 and KC == 2 and TC == 2 and KROWS <= P

    x_v = x.rearrange("b (c p) d -> b p c d", p=P)
    c_v = ctx_in.rearrange("b (c p) d -> b p c d", p=P)
    m_v = mask.rearrange("b o u (c p) -> b (o u p) c", p=P)
    out_v = out.rearrange("b (c p) d -> b p c d", p=P)
    out_rows = out.rearrange("b s d -> (b s) d")

    split_d = nc.dram_tensor("split_d", (RING, 2, 3, H * DEP, S), BF16, kind="Internal").ap()
    maskp_d = nc.dram_tensor("maskp_d", (B, 3, S), BF16, kind="Internal").ap()
    negmax_d = nc.dram_tensor("negmax_d", (RING, 6, H, S), BF16, kind="Internal").ap()
    slots_d = nc.dram_tensor("slots_d", (T, ROW), F32, kind="Internal").ap()

    with ExitStack() as es:
        def sb(name, shape, dt=F32):
            return es.enter_context(nc.sbuf_tensor(name, shape, dt))

        def sem(name):
            return es.enter_context(nc.semaphore(name))

        w_sb = {n: sb(f"w{n}", [P, KC, D]) for n in "qkvo"}
        wg_sb = sb("wg_sb", [P, KC, E])
        bias_qk = sb("bias_qk", [P, 2, KC])
        bv_sb = sb("bv_sb", [P, D])
        bo_sb = sb("bo_sb", [P, D])
        ident = sb("ident", [P, P])
        tri = sb("tri", [P, P], BF16)
        onesm = sb("onesm", [P, P], BF16)
        expo = sb("expo", [P, TC])
        iota8 = sb("iota8", [P, TC, E])
        ones_row = sb("ones_row", [3, H * S], BF16)
        mask_i = sb("mask_i", [B, S], I32)
        mask_f = sb("mask_f", [B, S])
        mask_p = sb("mask_p", [B, 3, S], BF16)
        x_sb = sb("x_sb", [P, RING, TC, D])
        c_sb = sb("c_sb", [P, RING, TC, D])
        st1 = sb("st1", [P, TC, 6])
        mv1 = sb("mv1", [P, TC, 2])
        rs1 = sb("rs1", [P, 2, TC])
        xn = sb("xn", [P, TC, D])
        xnT = sb("xnT", [P, KC, S])
        cT = sb("cT", [P, RING, KC, S])
        qk = sb("qk", [P, 2, KC, S])
        parts = sb("parts", [P, 2, 3, KC, S], BF16)
        qs = sb("qs", [P, RING, H, S], BF16)
        ks = sb("ks", [P, RING, H, S], BF16)
        v_sb = sb("v_sb", [P, RING, TC, H, 32])
        mx = sb("mx", [P, H, TC])
        nm = sb("nm", [HH, 2, S])
        zeros = sb("zeros", [P, KC * S])
        nmp = sb("nmp", [HH, 2, 3, S], BF16)
        mask_c = sb("mask_c", [P, RING, TC], I32)
        mbias = sb("mbias", [P, RING, TC])
        probs = sb("probs", [P, 4, 2 * S])
        av = sb("av", [P, 2, 2, S])
        rec = sb("rec", [P, 2, TC, HH])
        an = sb("an", [P, TC, D])
        anT = sb("anT", [P, KC, S])
        xr = sb("xr", [P, RING, TC, D])
        rows = sb("rows", [P, RING, TC, ROW])
        st2 = sb("st2", [P, TC, 6])
        mv2 = sb("mv2", [P, TC, 2])
        rs2 = sb("rs2", [P, TC])
        x2n = sb("x2n", [P, TC, D])
        x2T = sb("x2T", [P, KC, S])
        lg = sb("lg", [P, TC, E])
        top = sb("top", [P, TC, 8])
        topi = sb("topi", [P, TC, 8], U32)
        expf = sb("expf", [P, TC])
        oh = sb("oh", [P, TC, E], BF16)
        seen = sb("seen", [P, TC + 1, E], BF16)
        ld = sb("ld", [P, TC, E])
        le = sb("le", [P, TC, E])
        lsum = sb("lsum", [P, TC])
        loc = sb("loc", [P, TC, E])
        locv = sb("locv", [P, TC])
        slotf = sb("slotf", [P, TC])
        late = sb("late", [P, TC])
        tokf = sb("tokf", [P, TC])
        sloti = sb("sloti", [P, RING, TC], U32)
        g_rows = sb("g_rows", [P, GR, GT, ROW])
        g_flat = g_rows[:, :, :, :].rearrange("p e g r -> p (e g r)")
        w_in = g_flat[:, 0:E * KC * D].rearrange("p (e c h) -> p e c h", e=E, c=KC)
        far = g_flat[:, E * KC * D:E * KC * D + FARR * ROW]
        zero_row = probs[0:3].rearrange("p s t -> p (s t)").bitcast(BF16)
        be_sb = sb("be_sb", [P, E, D])
        weT = sb("weT", [P, E, KC, D])
        spare = [ks[:, s].rearrange("p h t -> p (h t)").bitcast(F32) for s in range(RING)]
        g_n = spare[0].rearrange("p (s g n) -> p s g n", s=2, g=GT)
        g_T = spare[1].rearrange("p (s r c t) -> p s r c t", s=2, r=2, c=KC)
        g_out = spare[2].rearrange("p (s g n) -> p s g n", s=2, g=GT)
        g_y = sb("g_y", [P, 2, D])
        g_tok = sb("g_tok", [P, E, GT], U32)

        bank = [es.enter_context(nc.psum_tensor(f"bank{n}", [P, 512], F32)) for n in range(8)]
        P1, P2, CB, M = bank[0:2], bank[2:5], bank[5], bank[6:8]

        wqk_landed = sem("wqk_landed")
        w_landed = sem("w_landed")
        we_landed = sem("we_landed")
        far_out = sem("far_out")
        mask_landed = sem("mask_landed")
        maskp_out = sem("maskp_out")
        const_out = sem("const_out")
        x_landed = [sem(f"x_landed{s}") for s in range(RING)]
        c_landed = [sem(f"c_landed{s}") for s in range(RING)]
        mc_landed = [sem(f"mc_landed{s}") for s in range(RING)]
        xr_landed = [sem(f"xr_landed{s}") for s in range(RING)]
        split_out = [sem(f"split_out{s}") for s in range(RING)]
        stack_landed = [sem(f"stack_landed{s}") for s in range(RING)]
        nm_out = [sem(f"nm_out{h}") for h in range(2)]
        nm_landed = [[sem(f"nm_landed{h}_{s}") for s in range(RING)] for h in range(2)]
        store_out = [sem(f"store_out{s}") for s in range(RING)]
        scat_out = [sem(f"scat_out{s}") for s in range(RING)]
        g_landed = [sem(f"g_landed{e}") for e in range(E)]
        y_out = [sem(f"y_out{s}") for s in range(2)]
        pool_const = sem("pool_const")
        dve_const = sem("dve_const")
        TASKS = ["MTb", "CT", "C2T", "XT", "NT", "K", "O", "Q", "MTa", "V", "X2T", "C1T", "R", "L"]
        made = {t: sem(f"made_{t}") for t in TASKS}
        took = {t: sem(f"took_{t}") for t in TASKS}
        ln1_chain = sem("ln1_chain")
        rs1_chain = sem("rs1_chain")
        xn_ready = sem("xn_ready")
        high_done = {t: sem(f"high_done_{t}") for t in "QK"}
        mid_done = {t: sem(f"mid_done_{t}") for t in "QK"}
        split_done = sem("split_done")
        nm_high = [sem("nm_high0"), sem("nm_high1")]
        p1_ready = sem("p1_ready")
        max_done = sem("max_done")
        nm_chain = [sem("nm_chain0"), sem("nm_chain1")]
        p2_ready = sem("p2_ready")
        exp_done = sem("exp_done")
        pv_done = sem("pv_done")
        av_ready = [sem("av_ready0"), sem("av_ready1")]
        mbias_ready = sem("mbias_ready")
        rec_done = [sem("rec_done0"), sem("rec_done1")]
        xr_ready = sem("xr_ready")
        ln2_chain = sem("ln2_chain")
        rs2_chain = sem("rs2_chain")
        x2n_ready = sem("x2n_ready")
        route = sem("route")
        le_ready = sem("le_ready")
        rows_ready = sem("rows_ready")
        passed = sem("passed")
        we_T = sem("we_T")
        weT_ready = sem("weT_ready")
        gn_ready = sem("gn_ready")
        gT_made = sem("gT_made")
        gT_ready = sem("gT_ready")
        y_made = sem("y_made")
        y_chain = sem("y_chain")
        gtok_ready = sem("gtok_ready")

        ROUTE1, ROUTE2 = 11, 6
        ROUTE = ROUTE1 + ROUTE2
        STACK_DMAS = 2 * len(PAIRS) + 2
        STAGE = {"XT": 3, "CT": 3, "K": 3, "Q": 3, "V": 1, "MTa": 1, "MTb": 0, "C1T": 0,
                 "C2T": -1, "NT": -1, "O": -1, "X2T": -1, "R": -1, "L": -1}
        WTURN = {-3: range(0, E // 2), -2: range(E // 2, E)}
        FULL = range(1, B - 3)
        assert len(FULL) % RING == 0

        def g_bank(e, r):
            return ((P2[0], P2[1]), (P2[2], CB))[e % 2][r]

        def bank_of(task):
            return M[TASKS.index(task) % 2]

        def has(stage, i, known):
            return True if known is None else 0 <= known + stage < B

        def wait(eng, s, value):
            if isinstance(value, int) and value <= 0:
                return
            eng.wait_ge(s, value)

        def apart(eng):
            eng.sem_inc(passed, 1)

        def claim(pe, task, i, known):
            order = [t for t in TASKS if bank_of(t) is bank_of(task)]
            n = order.index(task)
            back = 0
            while True:
                n -= 1
                if n < 0:
                    n, back = len(order) - 1, back + 1
                if known is not None and known - back < -3:
                    return
                t = order[n]
                if known is None and back and STAGE[t] < 0:
                    return
                if has(STAGE[t], i, None if known is None else known - back):
                    wait(pe, took[t], i - back + STAGE[t] + 1)
                    return

        def slot_of(slot, stage):
            return (slot + stage) % RING

        block = es.enter_context(nc.Block())

        def looped(eng, turn):
            for i in range(-3, FULL[0]):
                turn(i, i, i % RING, lambda st, i=i: (i + st) // RING + 1)
            with eng.Fori(0, len(FULL) // RING) as j:
                for u in range(RING):
                    c = u + FULL[0]
                    turn(j * RING + c, None, c % RING, lambda st, c=c: j + ((c + st) // RING + 1))
            for i in range(FULL[-1] + 1, B + 1):
                turn(i, i, i % RING, lambda st, i=i: (i + st) // RING + 1)

        @block.sync
        def _(sp):
            for b in range(RING):
                sp.dma_start(x_sb[:, b], x_v[b]).then_inc(x_landed[b], 16)
                sp.dma_start(c_sb[:, b], c_v[b]).then_inc(c_landed[b], 16)
            sp.wait_ge(dve_const, 2)
            for s in range(RING):
                sp.dma_start(negmax_d[s, 0:3].rearrange("r h t -> r (h t)"), zero_row).then_inc(const_out, 16)
                sp.dma_start(ks[XROW:KROWS, s].rearrange("r h t -> r (h t)"), ones_row[:, :]).then_inc(const_out, 16)
            sp.wait_ge(dve_const, 7)
            sp.dma_start(maskp_d, mask_p[:, :, :]).then_inc(maskp_out, 16)
            sp.wait_ge(maskp_out, 16)

            def negmax_rows(half, b, s, rnd_b):
                hs = slice(half * HH, (half + 1) * HH)
                wait(sp, nm_chain[half], 2 * (b + 1))
                apart(sp)
                sp.dma_start(negmax_d[s, 3:6, hs].rearrange("r h t -> h r t"), nmp[:, half]).then_inc(nm_out[half], 16)
                wait(sp, nm_out[half], 16 * (b + 1))
                apart(sp)
                sp.dma_start(qs[MROW:KROWS, s, hs].rearrange("r h t -> r (h t)"),
                             negmax_d[s, :, hs].rearrange("r h t -> r (h t)")).then_inc(nm_landed[half][s], 16)

            def turn(i, known, slot, rnd):
                if has(3, i, known) and not (known is not None and known + 3 < RING):
                    s = slot_of(slot, 3)
                    wait(sp, xn_ready, i + 1)
                    apart(sp)
                    sp.dma_start(x_sb[:, s], x_v[i + 3]).then_inc(x_landed[s], 16)
                    wait(sp, made["CT"], i + 1)
                    apart(sp)
                    sp.dma_start(c_sb[:, s], c_v[i + 3]).then_inc(c_landed[s], 16)
                if has(-1, i, known):
                    s = slot_of(slot, -1)
                    wait(sp, max_done, H * i)
                    apart(sp)
                    sp.dma_start(xr[:, s], x_v[i - 1]).then_inc(xr_landed[s], 16)
                if has(1, i, known):
                    s = slot_of(slot, 1)
                    wait(sp, max_done, H * i)
                    apart(sp)
                    sp.dma_start(mask_c[:, s], m_v[i + 1], allow_slow_non_contiguous=True).then_inc(mc_landed[s], 16)
                if has(2, i, known):
                    s = slot_of(slot, 2)
                    wait(sp, split_done, 2 * (i + 3))
                    apart(sp)
                    wait(sp, stack_landed[s], 16 * STACK_DMAS * (rnd(2) - 1))
                    apart(sp)
                    sp.dma_start(split_d[s].rearrange("e r (c p) t -> p (e r c) t", p=P),
                                 parts[:, :, :, :, :].rearrange("p e r c t -> p (e r c) t")).then_inc(split_out[s], 16)
                if has(0, i, known):
                    negmax_rows(1, i, slot, rnd(0))
                if has(2, i, known):
                    s = slot_of(slot, 2)
                    wait(sp, split_out[s], 16 * rnd(2))
                    apart(sp)
                    wait(sp, p2_ready, H * i)
                    apart(sp)
                    for side, stack in ((0, qs), (1, ks)):
                        src = split_d[s, side].rearrange("r (h d) t -> r d h t", d=DEP)
                        for n, pair in enumerate(PAIRS):
                            sp.dma_start(stack[n * DEP:(n + 1) * DEP, s], src[pair[side]]).then_inc(stack_landed[s], 16)
                    sp.dma_start(qs[MROW:MROW + 3, s].rearrange("r h t -> r (h t)"), ones_row[:, :]).then_inc(stack_landed[s], 16)
                    sp.dma_start(ks[MROW:MROW + 3, s], maskp_d[i + 2].rearrange("r (o t) -> r o t", o=1).to_broadcast([3, H, S])
                                 ).then_inc(stack_landed[s], 16)
                if has(1, i, known):
                    negmax_rows(0, i + 1, slot_of(slot, 1), rnd(1))
                if has(-1, i, known):
                    s = slot_of(slot, -1)
                    wait(sp, took["O"], i)
                    apart(sp)
                    sp.dma_start(out_v[i - 1], rows[:, s, :, 0:D]).then_inc(store_out[s], 16)

            looped(sp, turn)

            for s in range(RING):
                n = len(range(s, B, RING))
                sp.wait_ge(scat_out[s], 32 * (n + 1))
            slots_v = slots_d.rearrange("(e g p) c -> e p g c", e=E, p=P)
            for e in range(E):
                if e >= GR:
                    sp.wait_ge(y_chain, 4 * (e - GR + 1))
                sp.dma_start(g_rows[:, e % GR], slots_v[e]).then_inc(g_landed[e], 16)
            for s in range(2):
                sp.wait_ge(y_out[s], 16 * GT * (E // 2))

        @block.gpsimd
        def _(pool):
            g = nc.gpsimd
            for s in range(RING):
                pool.sem_inc(store_out[s], 16)
            g.memset(far, FAR).then_inc(pool_const, 1)
            g.memset(expo[:, :], -0.5).then_inc(pool_const, 1)
            g.memset(ident[:, :], 0.0).then_inc(pool_const, 1)
            g.memset(tri[:, :], 1.0).then_inc(pool_const, 1)
            pool.wait_ge(pool_const, 4)
            g.affine_select(out=ident[:, :], in_=ident[:, :], compare_op=ALU.not_equal, fill=1.0,
                            base=0, pattern=[[-1, P]], channel_multiplier=1).then_inc(pool_const, 1)
            g.affine_select(out=tri[:, :], in_=tri[:, :], compare_op=ALU.is_gt, fill=0.0,
                            base=0, pattern=[[1, P]], channel_multiplier=-1).then_inc(pool_const, 1)
            g.iota(iota8[:, :, :], pattern=[[0, TC], [1, E]], base=0, channel_multiplier=0,
                   allow_small_or_imprecise_dtypes=True).then_inc(pool_const, 1)
            g.iota(tokf[:, :], pattern=[[P, TC]], base=-S, channel_multiplier=1,
                   allow_small_or_imprecise_dtypes=True).then_inc(pool_const, 1)

            def negmax_parts(half, b):
                c = nm_chain[half]
                pool.wait_ge(took["MTb" if half else "MTa"], b + 1)
                apart(pool)
                g.tensor_tensor(nmp[:, half, 1], nm[:, half], zeros[0:HH, 0:S], ALU.add).then_inc(c, 1)
                pool.wait_ge(c, 2 * b + 1)
                apart(pool)
                g.tensor_tensor(nmp[:, half, 2], nm[:, half], nmp[:, half, 1], ALU.subtract).then_inc(c, 1)

            def low_part(task, b):
                side = 1 if task == "K" else 0
                pool.wait_ge(mid_done[task], b + 1)
                apart(pool)
                g.tensor_tensor(parts[:, side, 2], qk[:, side], parts[:, side, 1], ALU.subtract).then_inc(split_done, 1)

            def turn(i, known, slot, rnd):
                if known == -1:
                    far_v = slots_d.rearrange("(n p r) c -> n p (r c)", p=P, r=FARR)
                    for n in range(FARS):
                        g.dma_start(far_v[n], far).then_inc(scat_out[n // 2] if n < 2 * RING else far_out, 16)
                if has(3, i, known):
                    pool.wait_ge(ln1_chain, 4 * (i + 4))
                    apart(pool)
                    g.tensor_scalar(rs1[:, 0], mv1[:, :, 1], EPS, None, ALU.add).then_inc(rs1_chain, 1)
                    pool.wait_ge(rs1_chain, 2 * (i + 3) + 1)
                    apart(pool)
                    g.tensor_tensor(rs1[:, 1], rs1[:, 0], expo[:, :], ALU.pow).then_inc(rs1_chain, 1)
                if has(0, i, known):
                    negmax_parts(1, i)
                if has(-1, i, known):
                    s = slot_of(slot, -1)
                    pool.wait_ge(xr_landed[s], 16 * rnd(-1))
                    apart(pool)
                    g.tensor_tensor(xr[:, s], xr[:, s], bo_sb[:, :].rearrange("p (o n) -> p o n", o=1).to_broadcast([P, TC, D]),
                                    ALU.add).then_inc(xr_ready, 1)
                    pool.wait_ge(ln2_chain, 4 * i)
                    apart(pool)
                    g.tensor_scalar(rs2[:, :], mv2[:, :, 1], EPS, None, ALU.add).then_inc(rs2_chain, 1)
                    pool.wait_ge(rs2_chain, 3 * (i - 1) + 1)
                    apart(pool)
                    g.tensor_tensor(rows[:, s, :, RSTD], rs2[:, :], expo[:, :], ALU.pow).then_inc(rs2_chain, 1)
                    g.tensor_copy(rows[:, s, :, MEAN], mv2[:, :, 0]).then_inc(rs2_chain, 1)
                if has(3, i, known):
                    low_part("K", i + 3)
                if has(1, i, known):
                    negmax_parts(0, i + 1)
                if has(3, i, known):
                    low_part("Q", i + 3)
                if has(-1, i, known):
                    s = slot_of(slot, -1)
                    pool.wait_ge(rows_ready, i)
                    apart(pool)
                    for t in range(TC):
                        g.indirect_dma_start(slots_d, bass.IndirectOffsetOnAxis(ap=sloti[:, s, t:t + 1], axis=0),
                                             rows[:, s, t, :], None, bounds_check=T - 1, oob_is_err=False
                                             ).then_inc(scat_out[s], 16)

                if known == 0:
                    pool.wait_ge(w_landed, 16 * 5)
                    pool.wait_ge(far_out, 16 * (FARS - 2 * RING))
                    for n in range(RING):
                        pool.wait_ge(scat_out[n], 32)

            looped(pool, turn)

            for s in range(RING):
                pool.wait_ge(store_out[s], 16 * (len(range(s, B, RING)) + 1))
            for e in range(E):
                for t in range(GT):
                    if t % 2 == 0:
                        pool.wait_ge(y_chain, 4 * e + 2 * (t // 2 + 1))
                    g.indirect_dma_start(out_rows, bass.IndirectOffsetOnAxis(ap=g_tok[:, e, t:t + 1], axis=0),
                                         g_out[:, e % 2, t, :], None, bounds_check=T - 1, oob_is_err=False
                                         ).then_inc(y_out[e % 2], 16)

        @block.scalar
        def _(act):
            a = nc.scalar

            def evac(task, b, dst):
                act.wait_ge(made[task], b + 1)
                a.activation(dst, bank_of(task)[:, :], ACT.Copy).then_inc(took[task], 1)

            def high_part(task, b, prev_out):
                side = 1 if task == "K" else 0
                act.wait_ge(made[task], b + 1)
                if prev_out is not None:
                    wait(act, *prev_out)
                for c in range(KC):
                    r = a.activation(parts[:, side, 0, c], bank_of(task)[:, c * S:(c + 1) * S], ACT.Identity,
                                     bias=bias_qk[:, side, c:c + 1])
                r.then_inc(high_done[task], 1)

            def mid_part(task, b):
                side = 1 if task == "K" else 0
                act.wait_ge(took[task], b + 1)
                a.activation(parts[:, side, 1], qk[:, side], ACT.Copy).then_inc(mid_done[task], 1)

            def neg_evac(task, half, b):
                act.wait_ge(made[task], b + 1)
                wait(act, nm_out[half], 16 * b)
                a.activation(nmp[:, half, 0], bank_of(task)[0:HH, 0:S], ACT.Copy, scale=-1.0).then_inc(nm_high[half], 1)

            def sums_evac(half, b, quads):
                act.wait_ge(pv_done, quads)
                wait(act, made["C1T"], b + half)
                a.activation(av[:, half], CB[:, :].rearrange("p (g t) -> p g t", g=2), ACT.Copy).then_inc(av_ready[half], 1)

            def weights(e):
                act.wait_ge(we_T, e + 1)
                a.activation(weT[:, e].rearrange("p c f -> p (c f)"), CB[:, :] if e % 2 else P2[0][:, :], ACT.Copy).then_inc(weT_ready, 1)

            for n, w in (("k", wk), ("q", wq)):
                act.dma_start(w_sb[n][:, :, :], w.rearrange("(c p) n -> p c n", p=P)).then_inc(wqk_landed, 16)
            for n, v in enumerate((bq, bk)):
                act.dma_start(bias_qk[:, n, :], v.rearrange("(c p) -> p c", p=P),
                              allow_slow_non_contiguous=True).then_inc(wqk_landed, 16)
            act.dma_start(mask_i[:, :], mask.rearrange("b o u s -> (b o u) s")).then_inc(mask_landed, 16)
            act.dma_start(w_in[:, :, :, :], w_exp.rearrange("e (c p) h -> p e c h", p=P)).then_inc(we_landed, 16)
            for n, w in (("v", wv), ("o", wo)):
                act.dma_start(w_sb[n][:, :, :], w.rearrange("(c p) n -> p c n", p=P)).then_inc(w_landed, 16)
            act.dma_start(wg_sb[:, :, :], wg.rearrange("(c p) e -> p c e", p=P)).then_inc(w_landed, 16)
            for t, v in ((bv_sb, bv), (bo_sb, bo)):
                act.dma_start(t[:, :], v.rearrange("(o n) -> o n", o=1).to_broadcast([P, D])).then_inc(w_landed, 16)
            act.dma_start(be_sb[:, :, :], b_exp.rearrange("(o e) d -> o e d", o=1).to_broadcast([P, E, D])).then_inc(we_landed, 16)

            def turn(i, known, slot, rnd):
                for k in range(QUADS):
                    if has(0, i, known):
                        if k == 0:
                            act.wait_ge(mbias_ready, i + 1)
                        c = k % 2
                        for n in (2 * k, 2 * k + 1):
                            act.wait_ge(p2_ready, H * i + (n + 1))
                            wait(act, pv_done, QUADS * i + (n // 2 - 1))
                            a.activation(probs[:, n % 4], P2[(slot * H + n) % 3][:, :], ACT.Exp,
                                         bias=mbias[:, slot, c:c + 1], scale=SCALE).then_inc(exp_done, 1)
                    if k == 0 and has(-1, i, known):
                        sums_evac(1, i - 1, QUADS * i)
                    if k == 0 and has(0, i, known):
                        neg_evac("MTb", 1, i)
                    if k == 1 and has(3, i, known):
                        wait(act, made["V"], i + 1)
                        evac("CT", i + 3, cT[:, slot_of(slot, 3)].rearrange("p c t -> p (c t)"))
                    if k == 2 and has(3, i, known):
                        evac("XT", i + 3, xnT[:, :, :].rearrange("p c t -> p (c t)"))
                    if k == 2 and has(-1, i, known):
                        evac("NT", i - 1, anT[:, :, :].rearrange("p c t -> p (c t)"))
                    if k == 3 and has(3, i, known):
                        if known is not None:
                            act.wait_ge(wqk_landed, 16 * 4)
                        prev = (split_out[slot_of(slot, 2)], 16 * rnd(2)) if known is None or known + 2 >= 0 else None
                        high_part("K", i + 3, prev)
                    if k == 4 and has(3, i, known):
                        mid_part("K", i + 3)
                        high_part("Q", i + 3, None)
                    if k == 4 and has(1, i, known):
                        neg_evac("MTa", 0, i + 1)
                    if k == 4 and has(0, i, known):
                        sums_evac(0, i, QUADS * i + QUADS // 2)
                    if k == 5 and has(3, i, known):
                        mid_part("Q", i + 3)
                    if k == 5 and has(-1, i, known):
                        evac("X2T", i - 1, x2T[:, :, :].rearrange("p c t -> p (c t)"))
                    if k == 7 and has(-1, i, known):
                        act.wait_ge(route, ROUTE * (i - 1) + ROUTE1)
                        a.activation(le[:, :, :], ld[:, :, :], ACT.Exp).then_inc(le_ready, 1)
                if known is not None and known in WTURN:
                    for e in WTURN[known]:
                        weights(e)

            looped(act, turn)

            for e in range(E):
                for r in range(2):
                    act.wait_ge(gT_made, 2 * e + r + 1)
                    if e >= 2:
                        act.wait_ge(y_made, 2 * (e - 2) + r + 1)
                    a.activation(g_T[:, e % 2, r].rearrange("p c t -> p (c t)"), P1[r][:, :], ACT.Copy).then_inc(gT_ready, 1)

        @block.vector
        def _(dve):
            v = nc.vector
            v.memset(ones_row[:, :], 1.0).then_inc(dve_const, 1)
            v.memset(zero_row, 0.0).then_inc(dve_const, 1)
            v.memset(onesm[:, :], 1.0)
            v.memset(zeros[:, :], 0.0)
            v.memset(seen[:, :, :], 0.0)
            for s in range(RING):
                v.memset(v_sb[:, s], 1.0)
            dve.wait_ge(mask_landed, 16)
            v.tensor_scalar(mask_f[:, :], mask_i[:, :], NEG / SCALE, None, ALU.mult).then_inc(dve_const, 1)
            dve.wait_ge(dve_const, 3)
            v.tensor_copy(mask_p[:, 0], mask_f[:, :]).then_inc(dve_const, 1)
            dve.wait_ge(dve_const, 4)
            v.tensor_tensor(mask_f[:, :], mask_f[:, :], mask_p[:, 0], ALU.subtract).then_inc(dve_const, 1)
            dve.wait_ge(dve_const, 5)
            v.tensor_copy(mask_p[:, 1], mask_f[:, :]).then_inc(dve_const, 1)
            dve.wait_ge(dve_const, 6)
            v.tensor_tensor(mask_p[:, 2], mask_f[:, :], mask_p[:, 1], ALU.subtract).then_inc(dve_const, 1)
            dve.wait_ge(pool_const, 8)

            def normalise(task, half, b):
                src = bank_of(task)[:, :].rearrange("p (q h e) -> p q h e", q=TC, e=32)
                dve.wait_ge(made[task], b + 1)
                v.reciprocal(rec[:, half], src[:, :, :, DEP]).then_inc(rec_done[half], 1)
                dve.wait_ge(rec_done[half], b + 1)
                if half == 0:
                    wait(dve, made["NT"], b)
                v.tensor_tensor(an[:, :, half * P:(half + 1) * P].rearrange("p q (h d) -> p q h d", d=DEP),
                                src[:, :, :, 0:DEP],
                                rec[:, half].rearrange("p q (h o) -> p q h o", o=1).to_broadcast([P, TC, HH, DEP]),
                                ALU.mult).then_inc(took[task], 1)

            def rest(task, b):
                side = 1 if task == "K" else 0
                dve.wait_ge(high_done[task], b + 1)
                wait(dve, split_done, 2 * b)
                for c in range(KC):
                    r = v.scalar_tensor_tensor(out=qk[:, side, c], in0=bank_of(task)[:, c * S:(c + 1) * S],
                                               scalar=bias_qk[:, side, c:c + 1], in1=parts[:, side, 0, c],
                                               op0=ALU.add, op1=ALU.subtract)
                r.then_inc(took[task], 1)

            def neg_rest(task, half, b):
                dve.wait_ge(nm_high[half], b + 1)
                wait(dve, nm_chain[half], 2 * b)
                v.scalar_tensor_tensor(out=nm[:, half], in0=bank_of(task)[0:HH, 0:S], scalar=-1.0,
                                       in1=nmp[:, half, 0], op0=ALU.mult, op1=ALU.subtract).then_inc(took[task], 1)

            def statistics(src, st, mv, chain, b):
                for t in range(TC):
                    v.bn_stats(st[:, t], src[:, t]).then_inc(chain, 1)
                for t in range(TC):
                    dve.wait_ge(chain, 4 * b + t + 1)
                    apart(dve)
                    v.bn_aggr(mv[:, t], st[:, t]).then_inc(chain, 1)

            def turn(i, known, slot, rnd):
                sp1 = slot_of(slot, -1)
                for k in range(QUADS):
                    if has(1, i, known):
                        for h in (2 * k, 2 * k + 1):
                            dve.wait_ge(p1_ready, H * (i + 1) + (h + 1))
                            if h == 0:
                                wait(dve, made["MTa"], i + 1)
                            if h == HH:
                                wait(dve, made["MTb"], i + 1)
                            v.tensor_reduce(mx[:, h], P1[h % 2][:, :].rearrange("p (q t) -> p q t", q=TC),
                                            AX.X, ALU.max).then_inc(max_done, 1)
                    if k == 0 and has(3, i, known):
                        dve.wait_ge(x_landed[slot_of(slot, 3)], 16 * rnd(3))
                        statistics(x_sb[:, slot_of(slot, 3)], st1, mv1, ln1_chain, i + 3)
                    if k == 3 and has(1, i, known):
                        s = slot_of(slot, 1)
                        dve.wait_ge(mc_landed[s], 16 * rnd(1))
                        wait(dve, exp_done, H * i)
                        v.tensor_scalar(mbias[:, s], mask_c[:, s], NEG, None, ALU.mult).then_inc(mbias_ready, 1)
                    if k == 0 and has(0, i, known):
                        neg_rest("MTb", 1, i)
                    if k == 1 and has(-1, i, known):
                        normalise("C2T", 1, i - 1)
                    if k == 1 and has(3, i, known):
                        dve.wait_ge(rs1_chain, 2 * (i + 4))
                        wait(dve, made["XT"], i + 3)
                        for t in range(TC):
                            r = v.tensor_scalar(xn[:, t], x_sb[:, slot_of(slot, 3), t], mv1[:, t, 0:1],
                                                rs1[:, 1, t:t + 1], ALU.subtract, ALU.mult)
                        r.then_inc(xn_ready, 1)
                    if k == 3 and has(-1, i, known):
                        dve.wait_ge(made["O"], i)
                        dve.wait_ge(xr_ready, i)
                        dve.wait_ge(store_out[sp1], 16 * rnd(-1))
                        dve.wait_ge(scat_out[sp1], 32 * rnd(-1))
                        v.tensor_tensor(rows[:, sp1, :, 0:D], bank_of("O")[:, :].rearrange("p (q n) -> p q n", q=TC),
                                        xr[:, sp1], ALU.add).then_inc(took["O"], 1)
                        dve.wait_ge(took["O"], i)
                        statistics(rows[:, sp1, :, 0:D], st2, mv2, ln2_chain, i - 1)
                    if k == 3 and has(3, i, known):
                        rest("K", i + 3)
                    if k == 4 and has(3, i, known):
                        rest("Q", i + 3)
                    if k == 4 and has(1, i, known):
                        neg_rest("MTa", 0, i + 1)
                    if k == 4 and has(-1, i, known):
                        dve.wait_ge(rs2_chain, 3 * i)
                        wait(dve, made["C1T"], i)
                        for t in range(TC):
                            r = v.tensor_scalar(x2n[:, t], rows[:, sp1, t, 0:D], rows[:, sp1, t, MEAN:MEAN + 1],
                                                rows[:, sp1, t, RSTD:RSTD + 1], ALU.subtract, ALU.mult)
                        r.then_inc(x2n_ready, 1)
                    if k == 5 and has(1, i, known):
                        s = slot_of(slot, 1)
                        dve.wait_ge(made["V"], i + 2)
                        if known is not None:
                            dve.wait_ge(w_landed, 16 * 5)
                        wait(dve, pv_done, QUADS * i)
                        v.tensor_tensor(v_sb[:, s, :, :, 0:DEP],
                                        bank_of("V")[:, :].rearrange("p (c h d) -> p c h d", c=TC, d=DEP),
                                        bv_sb[:, :].rearrange("p (o h d) -> p o h d", o=1, d=DEP).to_broadcast([P, TC, H, DEP]),
                                        ALU.add).then_inc(took["V"], 1)
                    if k == 5 and has(0, i, known):
                        normalise("C1T", 0, i)
                    if k == 6 and has(-1, i, known):
                        b = i - 1
                        n = [0]

                        def step(ins):
                            n[0] += 1
                            ins.then_inc(route, 1)

                        def steps_done():
                            dve.wait_ge(route, ROUTE * b + n[0])

                        dve.wait_ge(made["R"], i)
                        v.tensor_copy(lg[:, :, :], bank_of("R")[:, 0:TC * E].rearrange("p (q e) -> p q e", e=E)
                                      ).then_inc(took["R"], 1)
                        dve.wait_ge(took["R"], i)
                        apart(dve)
                        for t in range(TC):
                            step(v.max(top[:, t], lg[:, t]))
                        step(v.tensor_copy(seen[:, 0], seen[:, TC]))
                        steps_done()
                        apart(dve)
                        for t in range(TC):
                            step(v.max_index(topi[:, t], top[:, t], lg[:, t]))
                        step(v.tensor_tensor(ld[:, :, :], lg[:, :, :], top[:, :, 0:1].to_broadcast([P, TC, E]), ALU.subtract))
                        steps_done()
                        step(v.tensor_copy(expf[:, :], topi[:, :, 0]))
                        steps_done()
                        step(v.tensor_tensor(oh[:, :, :], iota8[:, :, :],
                                             expf[:, :].rearrange("p (q o) -> p q o", o=1).to_broadcast([P, TC, E]), ALU.is_equal))
                        for t in range(TC):
                            steps_done()
                            step(v.tensor_tensor(seen[:, t + 1], seen[:, t], oh[:, t], ALU.add))
                        step(v.tensor_scalar(tokf[:, :], tokf[:, :], float(S), None, ALU.add))
                        assert n[0] == ROUTE1
                    if k == 7 and has(-1, i, known):
                        b = i - 1
                        n = [ROUTE1]

                        def step(ins):
                            n[0] += 1
                            ins.then_inc(route, 1)

                        def steps_done():
                            dve.wait_ge(route, ROUTE * b + n[0])

                        steps_done()
                        v.tensor_copy(rows[:, sp1, :, TOK], tokf[:, :])
                        dve.wait_ge(made["L"], i)
                        v.tensor_tensor(loc[:, :, :], bank_of("L")[:, 0:TC * E].rearrange("p (q e) -> p q e", e=E),
                                        oh[:, :, :], ALU.mult).then_inc(took["L"], 1)
                        dve.wait_ge(took["L"], i)
                        step(v.tensor_reduce(locv[:, :], loc[:, :, :], AX.X, ALU.add))
                        dve.wait_ge(le_ready, i)
                        step(v.tensor_reduce(lsum[:, :], le[:, :, :], AX.X, ALU.add))
                        steps_done()
                        step(v.tensor_scalar(late[:, :], locv[:, :], float(CAP), FAR, ALU.is_ge, ALU.mult))
                        step(v.scalar_tensor_tensor(out=slotf[:, :], in0=expf[:, :], scalar=float(CAP), in1=locv[:, :],
                                                    op0=ALU.mult, op1=ALU.add))
                        step(v.reciprocal(rows[:, sp1, :, GATE], lsum[:, :]))
                        steps_done()
                        step(v.tensor_tensor(slotf[:, :], slotf[:, :], late[:, :], ALU.add))
                        steps_done()
                        v.tensor_copy(sloti[:, sp1], slotf[:, :]).then_inc(rows_ready, 1)
                        assert n[0] == ROUTE

            looped(dve, turn)

            dve.wait_ge(we_landed, 32)

            def slots_normed(e):
                dve.wait_ge(g_landed[e], 16)
                if e >= 2:
                    dve.wait_ge(gT_made, 2 * (e - 1))
                for t in range(GT):
                    v.tensor_scalar(g_n[:, e % 2, t], g_rows[:, e % GR, t, 0:D], g_rows[:, e % GR, t, MEAN:MEAN + 1],
                                    g_rows[:, e % GR, t, RSTD:RSTD + 1], ALU.subtract, ALU.mult).then_inc(gn_ready, 1)

            slots_normed(0)
            for e in range(E):
                if e + 1 < E:
                    slots_normed(e + 1)
                if e >= 2:
                    dve.wait_ge(y_out[e % 2], 16 * GT * (e // 2))
                v.tensor_copy(g_tok[:, e], g_rows[:, e % GR, :, TOK])
                for r in range(2):
                    dve.wait_ge(y_made, 2 * e + r + 1)
                    if 2 * e + r:
                        dve.wait_ge(y_chain, 4 * e + 2 * r)
                    v.tensor_tensor(g_y[:, :, :], g_bank(e, r)[:, :].rearrange("p (q n) -> p q n", q=2),
                                    be_sb[:, e].rearrange("p (o n) -> p o n", o=1).to_broadcast([P, 2, D]),
                                    ALU.add).then_inc(y_chain, 1)
                    dve.wait_ge(y_chain, 4 * e + 2 * r + 1)
                    for q in range(2):
                        t = 2 * r + q
                        o = v.scalar_tensor_tensor(out=g_out[:, e % 2, t], in0=g_y[:, q], scalar=g_rows[:, e % GR, t, GATE:GATE + 1],
                                                   in1=g_rows[:, e % GR, t, 0:D], op0=ALU.mult, op1=ALU.add)
                    o.then_inc(y_chain, 1)

        @block.tensor
        def _(pe):
            t_ = nc.tensor
            pe.wait_ge(pool_const, 8)
            pe.wait_ge(dve_const, 7)

            def transposes(task, src, ready):
                o = bank_of(task)
                for c in range(2):
                    for t in range(2):
                        r = t_.transpose(o[:, c * S + t * P:c * S + (t + 1) * P], src(c, t), ident[:, :])
                r.then_inc(made[task], 1)

            def product(task, lhs, rhs):
                o = bank_of(task)
                for n in range(2):
                    for c in range(2):
                        r = t_.matmul(o[:, n * S:(n + 1) * S], lhs(c, n), rhs(c, n), start=(c == 0), stop=(c == 1))
                r.then_inc(made[task], 1)

            def times_v(i, known, k, slot):
                g, c = k // 2, k % 2
                pe.wait_ge(exp_done, H * i + (2 * k + 2))
                if k == 0:
                    pe.wait_ge(took["V"], i + 1)
                    wait(pe, av_ready[1], i)
                if k == QUADS // 2:
                    pe.wait_ge(av_ready[0], i + 1)
                for j in range(4):
                    n = 2 * k + j // 2
                    r = t_.matmul(CB[32 * j:32 * j + 32, (g % 2) * S:(g % 2 + 1) * S], v_sb[:, slot, c, 4 * g + j, :],
                                  probs[:, n % 4, (j % 2) * S:(j % 2 + 1) * S], start=(c == 0), stop=(c == 1))
                r.then_inc(pv_done, 1)

            def negmax(task, half, b, i, known):
                pe.wait_ge(max_done, H * b + HH * (half + 1))
                claim(pe, task, i, known)
                for q in range(TC):
                    r = t_.transpose(bank_of(task)[0:HH, q * P:(q + 1) * P], mx[:, half * HH:(half + 1) * HH, q], ident[:, :])
                r.then_inc(made[task], 1)

            def turn(i, known, slot, rnd):
                if known is not None and known == -3:
                    pe.wait_ge(wqk_landed, 16 * 4)
                if known is not None and known == -1:
                    pe.wait_ge(w_landed, 16 * 5)
                    pe.wait_ge(const_out, 16 * 2 * RING)
                for k in range(QUADS):
                    g, c = k // 2, k % 2
                    if has(0, i, known):
                        if k == 0:
                            pe.wait_ge(nm_landed[0][slot], 16 * rnd(0))
                        if k == QUADS // 2:
                            pe.wait_ge(nm_landed[1][slot], 16 * rnd(0))
                        for n in (2 * k, 2 * k + 1):
                            wait(pe, exp_done, H * i + (n - 2))
                            for j in range(2):
                                h = 4 * g + 2 * (n % 2) + j
                                r = t_.matmul(P2[(slot * H + n) % 3][:, j * S:(j + 1) * S],
                                              ks[0:KROWS, slot, h, c * P:(c + 1) * P], qs[0:KROWS, slot, h, :],
                                              start=True, stop=True)
                            r.then_inc(p2_ready, 1)
                    if has(1, i, known):
                        s = slot_of(slot, 1)
                        if k == 0:
                            pe.wait_ge(stack_landed[s], 16 * STACK_DMAS * rnd(1))
                        for h in (2 * k, 2 * k + 1):
                            wait(pe, max_done, H * (i + 1) + (h - 1))
                            for q in range(TC):
                                r = t_.matmul(P1[h % 2][:, q * S:(q + 1) * S], qs[0:XROW, s, h, q * P:(q + 1) * P],
                                              ks[0:XROW, s, h, :], start=True, stop=True)
                            r.then_inc(p1_ready, 1)
                    if k > 0 and has(0, i, known):
                        times_v(i, known, k - 1, slot)
                    if k == 0 and has(-1, i, known):
                        times_v(i - 1, known, QUADS - 1, slot_of(slot, -1))
                    if k == 0 and has(0, i, known):
                        negmax("MTb", 1, i, i, known)
                    if k == 1 and has(3, i, known):
                        s = slot_of(slot, 3)
                        pe.wait_ge(c_landed[s], 16 * rnd(3))
                        claim(pe, "CT", i, known)
                        transposes("CT", lambda cc, t: c_sb[:, s, t, cc * P:(cc + 1) * P], None)
                    if k == 1 and has(-1, i, known):
                        pe.wait_ge(av_ready[1], i)
                        claim(pe, "C2T", i, known)
                        transposes("C2T", lambda q, gg: av[:, 1, gg, q * P:(q + 1) * P], None)
                    if k == 2 and has(3, i, known):
                        pe.wait_ge(xn_ready, i + 4)
                        claim(pe, "XT", i, known)
                        transposes("XT", lambda cc, t: xn[:, t, cc * P:(cc + 1) * P], None)
                    if k == 2 and has(-1, i, known):
                        pe.wait_ge(took["C2T"], i)
                        claim(pe, "NT", i, known)
                        transposes("NT", lambda cc, t: an[:, t, cc * P:(cc + 1) * P], None)
                    if k == 3 and has(3, i, known):
                        s = slot_of(slot, 3)
                        pe.wait_ge(took["CT"], i + 4)
                        claim(pe, "K", i, known)
                        product("K", lambda cc, n: w_sb["k"][:, cc, n * P:(n + 1) * P], lambda cc, n: cT[:, s, cc, :])
                    if k == 3 and has(-1, i, known):
                        pe.wait_ge(took["NT"], i)
                        claim(pe, "O", i, known)
                        product("O", lambda cc, n: anT[:, cc, n * P:(n + 1) * P], lambda cc, n: w_sb["o"][:, cc, :])
                    if k == 4 and has(3, i, known):
                        pe.wait_ge(took["XT"], i + 4)
                        claim(pe, "Q", i, known)
                        product("Q", lambda cc, n: w_sb["q"][:, cc, n * P:(n + 1) * P], lambda cc, n: xnT[:, cc, :])
                    if k == 4 and has(1, i, known):
                        negmax("MTa", 0, i + 1, i, known)
                    if k == 5 and has(1, i, known):
                        s1 = slot_of(slot, 1)
                        claim(pe, "V", i, known)
                        product("V", lambda cc, n: cT[:, s1, cc, n * P:(n + 1) * P], lambda cc, n: w_sb["v"][:, cc, :])
                    if k == 5 and has(-1, i, known):
                        pe.wait_ge(x2n_ready, i)
                        claim(pe, "X2T", i, known)
                        transposes("X2T", lambda cc, t: x2n[:, t, cc * P:(cc + 1) * P], None)
                    if k == 5 and has(0, i, known):
                        pe.wait_ge(av_ready[0], i + 1)
                        claim(pe, "C1T", i, known)
                        transposes("C1T", lambda q, gg: av[:, 0, gg, q * P:(q + 1) * P], None)
                    if k == 6 and has(-1, i, known):
                        pe.wait_ge(took["X2T"], i)
                        claim(pe, "R", i, known)
                        for t in range(TC):
                            for cc in range(KC):
                                r = t_.matmul(bank_of("R")[:, t * E:(t + 1) * E], x2T[:, cc, t * P:(t + 1) * P], wg_sb[:, cc, :],
                                              start=(cc == 0), stop=(cc == KC - 1))
                        r.then_inc(made["R"], 1)
                    if k == 7 and has(-1, i, known):
                        pe.wait_ge(route, ROUTE * (i - 1) + ROUTE1)
                        claim(pe, "L", i, known)
                        o = bank_of("L")[:, 0:TC * E]
                        t_.matmul(o, tri[:, :], oh[:, :, :].rearrange("p q e -> p (q e)"), start=True, stop=False)
                        t_.matmul(o, onesm[:, :], seen[:, 0:TC, :].rearrange("p q e -> p (q e)"), start=False, stop=True
                                  ).then_inc(made["L"], 1)
                if known is not None and known in WTURN:
                    pe.wait_ge(we_landed, 32)
                    for e in WTURN[known]:
                        if e >= 2:
                            pe.wait_ge(weT_ready, e - 1)
                        for c in range(KC):
                            for f in range(KC):
                                r = t_.transpose((CB if e % 2 else P2[0])[:, c * D + f * P:c * D + (f + 1) * P],
                                                 w_in[:, e, f, c * P:(c + 1) * P], ident[:, :])
                        r.then_inc(we_T, 1)

            looped(pe, turn)

            def slots_T(e):
                for r in range(2):
                    if e >= 1:
                        pe.wait_ge(gT_ready, 2 * (e - 1) + r + 1)
                    for q in range(2):
                        pe.wait_ge(gn_ready, GT * e + 2 * r + q + 1)
                        for c in range(KC):
                            o = t_.transpose(P1[r][:, c * S + q * P:c * S + (q + 1) * P],
                                             g_n[:, e % 2, 2 * r + q, c * P:(c + 1) * P], ident[:, :])
                    o.then_inc(gT_made, 1)

            pe.wait_ge(weT_ready, E)
            slots_T(0)
            for e in range(E):
                if e + 1 < E:
                    slots_T(e + 1)
                for r in range(2):
                    pe.wait_ge(gT_ready, 2 * e + r + 1)
                    if e >= 2:
                        pe.wait_ge(y_chain, 4 * (e - 2) + 2 * r + 1)
                    for q in range(2):
                        for c in range(KC):
                            o = t_.matmul(g_bank(e, r)[:, q * D:(q + 1) * D], g_T[:, e % 2, r, c, q * P:(q + 1) * P],
                                          weT[:, e, c, :], start=(c == 0), stop=(c == KC - 1))
                    o.then_inc(y_made, 1)


_INS = ["x", "ctx_1024", "mask_Bx1x1xS2_ik0", "L0_xattn_Wq", "L0_xattn_bq", "L0_xattn_Wk", "L0_xattn_bk",
        "L0_xattn_Wv", "L0_xattn_bv", "L0_xattn_Wo", "L0_xattn_bo", "L0_ffn_wg", "L0_ffn_W", "L0_ffn_b"]


def kernel(**inputs):
    import numpy as _np
    import concourse.bacc as _bacc
    from concourse import mybir as _mybir
    from concourse.bass_utils import run_bass_kernel_spmd as _run

    nc = _bacc.Bacc("TRN2", target_bir_lowering=False, num_devices=1)
    arrays, args = {}, []
    for name in _INS:
        a = _np.ascontiguousarray(inputs[name])
        arrays[f"in_{name}"] = a
        args.append(nc.dram_tensor(f"in_{name}", a.shape, _mybir.dt.from_np(a.dtype), kind="ExternalInput").ap())
    shape = inputs["x"].shape
    out = nc.dram_tensor("out_0", shape, _mybir.dt.float32, kind="ExternalOutput").ap()
    xattn_moe(nc, *args, out)
    r = _run(nc, [arrays], core_ids=[0])
    return r.results[0]["out_0"]
```

```python
from contextlib import ExitStack

import concourse.bass as bass
from concourse import mybir

P = 128
ALU = mybir.AluOpType
ACT = mybir.ActivationFunctionType
AX = mybir.AxisListType
F32 = mybir.dt.float32
F32R = mybir.dt.float32r
BF16 = mybir.dt.bfloat16
I32 = mybir.dt.int32
U32 = mybir.dt.uint32

RING = 3
EPS = 1e-5
NEG = -1e9
FAR = 1e6
PAIRS = [(0, 0), (0, 1), (1, 0), (0, 2), (2, 0), (1, 1)]


def xattn_moe(nc, x, ctx_in, mask, wq, bq, wk, bk, wv, bv, wo, bo, wg, w_exp, b_exp, out):
    B, S, D = x.shape
    E = wg.shape[1]
    T = B * S
    CAP = T // E
    H = 16
    DEP = D // H
    KC = D // P
    TC = S // P
    HH = H // 2
    QUADS = 2 * H // 4
    TERM = len(PAIRS) * DEP
    MROW = TERM
    XROW = TERM + 3
    KROWS = XROW + 3
    SCALE = float(DEP) ** -0.5
    ROW = D + 4
    MEAN, RSTD, GATE, TOK = D, D + 1, D + 2, D + 3
    GT = CAP // P
    FARR = 4
    FARS = T // (FARR * P)
    GR = 6
    assert E == QUADS
    assert S == 256 and D == 256 and KC == 2 and TC == 2 and KROWS <= P

    x_v = x.rearrange("b (c p) d -> b p c d", p=P)
    c_v = ctx_in.rearrange("b (c p) d -> b p c d", p=P)
    m_v = mask.rearrange("b o u (c p) -> b (o u p) c", p=P)
    out_v = out.rearrange("b (c p) d -> b p c d", p=P)
    out_rows = out.rearrange("b s d -> (b s) d")

    split_d = nc.dram_tensor("split_d", (RING, 2, 3, H * DEP, S), BF16, kind="Internal").ap()
    maskp_d = nc.dram_tensor("maskp_d", (B, 3, S), BF16, kind="Internal").ap()
    negmax_d = nc.dram_tensor("negmax_d", (RING, 6, H, S), BF16, kind="Internal").ap()
    slots_d = nc.dram_tensor("slots_d", (T, ROW), F32, kind="Internal").ap()

    with ExitStack() as es:
        def sb(name, shape, dt=F32):
            return es.enter_context(nc.sbuf_tensor(name, shape, dt))

        def sem(name):
            return es.enter_context(nc.semaphore(name))

        wg_sb = sb("wg_sb", [P, KC, E])
        bias_qk = sb("bias_qk", [P, 2, KC])
        bv_sb = sb("bv_sb", [P, KC])
        bv_wide = sb("bv_wide", [P, KC, P])
        bo_sb = sb("bo_sb", [P, D])
        ident = sb("ident", [P, P])
        tri = sb("tri", [P, P], BF16)
        onesm = sb("onesm", [P, P], BF16)
        expo = sb("expo", [P, TC])
        iota8 = sb("iota8", [P, TC, E])
        zero_row = sb("zero_row", [3, S], BF16)
        ones_row = sb("ones_row", [3, S], BF16)
        mask_i = sb("mask_i", [B, S], I32)
        mask_f = sb("mask_f", [B, S])
        mask_p = sb("mask_p", [B, 3, S], BF16)
        x_sb = sb("x_sb", [P, RING, TC, D])
        c_sb = sb("c_sb", [P, RING, TC, D])
        st1 = sb("st1", [P, TC, 6])
        mv1 = sb("mv1", [P, TC, 2])
        rs1 = sb("rs1", [P, 2, TC])
        xn = sb("xn", [P, TC, D])
        xnT = sb("xnT", [P, 2, KC, S], F32R)
        xnT_full = sb("xnT_full", [P, KC, S])
        cT = sb("cT", [P, RING, 2, KC, S], F32R)
        qk = sb("qk", [P, 2, KC, S])
        parts = sb("parts", [P, 2, 3, KC, S], BF16)
        qs = sb("qs", [P, RING, H, S], BF16)
        ks = sb("ks", [P, RING, H, S], BF16)
        v_sb = sb("v_sb", [P, RING, TC, H, 32])
        mx = sb("mx", [P, H, TC])
        nm = sb("nm", [HH, 2, S])
        zeros = sb("zeros", [P, KC * S])
        nmp = sb("nmp", [HH, 2, 3, S], BF16)
        mask_c = sb("mask_c", [P, RING, TC], I32)
        mbias = sb("mbias", [P, RING, TC])
        probs = sb("probs", [P, 4, 2 * S])
        av = sb("av", [P, 2, 2, S])
        rec = sb("rec", [P, 2, TC, HH])
        an = sb("an", [P, TC, D])
        anT = sb("anT", [P, 2, KC, S], F32R)
        xr = sb("xr", [P, RING, TC, D])
        rows = sb("rows", [P, RING, TC, ROW])
        st2 = sb("st2", [P, TC, 6])
        mv2 = sb("mv2", [P, TC, 2])
        rs2 = sb("rs2", [P, TC])
        x2n = sb("x2n", [P, TC, D])
        x2T = sb("x2T", [P, KC, S])
        lg = sb("lg", [P, TC, E])
        top = sb("top", [P, TC, 8])
        topi = sb("topi", [P, TC, 8], U32)
        expf = sb("expf", [P, TC])
        oh = sb("oh", [P, TC, E], BF16)
        seen = sb("seen", [P, E], BF16)
        ld = sb("ld", [P, TC, E])
        le = sb("le", [P, TC, E])
        lsum = sb("lsum", [P, TC])
        loc = sb("loc", [P, TC, E])
        locv = sb("locv", [P, TC])
        slotf = sb("slotf", [P, TC])
        late = sb("late", [P, TC])
        tokf = sb("tokf", [P, TC])
        batch_step = sb("batch_step", [P, TC])
        sloti = sb("sloti", [P, RING, TC], U32)
        g_rows = sb("g_rows", [P, GR, GT, ROW])
        w_part = g_rows[:, :, :, :].rearrange("p e g r -> p (e g r)")[:, 0:4 * 2 * KC * D].rearrange(
            "p (n r c d) -> p n r c d", n=4, r=2, c=KC).bitcast(F32R)
        w_in = qs[:, 1:3].rearrange("p s h t -> p (s h t)").bitcast(F32).rearrange("p (e c h) -> p e c h", e=E, c=KC)
        be_sb = sb("be_sb", [P, E, D])
        weT = sb("weT", [P, E, KC, D])
        w_raw = weT[:, 0:4]
        far = weT[:, 4:E].rearrange("p e c d -> p (e c d)")[:, 0:FARR * ROW]
        spare = [ks[:, s].rearrange("p h t -> p (h t)").bitcast(F32) for s in range(RING)]
        g_n = spare[0].rearrange("p (s g n) -> p s g n", s=2, g=GT)
        g_T = spare[1].rearrange("p (s r c t) -> p s r c t", s=2, r=2, c=KC)
        g_out = spare[2].rearrange("p (s g n) -> p s g n", s=2, g=GT)
        g_y = sb("g_y", [P, 2, D])
        g_tok = sb("g_tok", [P, E, GT], U32)

        bank = [es.enter_context(nc.psum_tensor(f"bank{n}", [P, 512], F32)) for n in range(8)]
        P1, P2, CB, M = bank[0:2], bank[2:4], bank[4], bank[5:8]

        wqk_landed = [sem("wk_landed"), sem("wq_landed")]
        bqk_landed = sem("bqk_landed")
        w_landed = sem("w_landed")
        w_high = sem("w_high")
        w_low = sem("w_low")
        we_landed = sem("we_landed")
        far_out = sem("far_out")
        mask_landed = sem("mask_landed")
        maskp_out = sem("maskp_out")
        const_out = sem("const_out")
        x_landed = [sem(f"x_landed{s}") for s in range(RING)]
        c_landed = [sem(f"c_landed{s}") for s in range(RING)]
        mc_landed = [sem(f"mc_landed{s}") for s in range(RING)]
        xr_landed = [sem(f"xr_landed{s}") for s in range(RING)]
        split_out = [[sem(f"split_out{n}_{s}") for s in range(RING)] for n in "QK"]
        stack_landed = [sem(f"stack_landed{s}") for s in range(RING)]
        nm_out = [sem(f"nm_out{h}") for h in range(2)]
        nm_landed = [[sem(f"nm_landed{h}_{s}") for s in range(RING)] for h in range(2)]
        store_out = [sem(f"store_out{s}") for s in range(RING)]
        scat_out = [sem(f"scat_out{s}") for s in range(RING)]
        g_landed = [sem(f"g_landed{e}") for e in range(E)]
        y_out = [sem(f"y_out{s}") for s in range(2)]
        pool_const = sem("pool_const")
        dve_const = sem("dve_const")
        BANK = {"MTb": 0, "CT": 2, "C2T": 1, "K": 0, "NT": 1, "XT": 2, "O": 1, "MTa": 0, "Q": 2, "C1T": 0,
                "X2T": 1, "R": 1, "V": 2, "L": 1}
        TASKS = list(BANK)
        made = {t: sem(f"made_{t}") for t in TASKS}
        high = {t: sem(f"high_{t}") for t in ("CT", "XT", "NT")}
        took = {t: sem(f"took_{t}") for t in TASKS}
        ln1_chain = sem("ln1_chain")
        rs1_chain = sem("rs1_chain")
        xn_ready = sem("xn_ready")
        xnT_ready = sem("xnT_ready")
        high_done = {t: sem(f"high_done_{t}") for t in "QK"}
        mid_done = {t: sem(f"mid_done_{t}") for t in "QK"}
        rest_done = {t: sem(f"rest_done_{t}") for t in "QK"}
        split_done = sem("split_done")
        nm_high = [sem("nm_high0"), sem("nm_high1")]
        p1_ready = sem("p1_ready")
        max_done = sem("max_done")
        nm_chain = [sem("nm_chain0"), sem("nm_chain1")]
        p2_ready = sem("p2_ready")
        exp_done = sem("exp_done")
        pv_done = sem("pv_done")
        av_ready = [sem("av_ready0"), sem("av_ready1")]
        mbias_ready = sem("mbias_ready")
        rec_done = [sem("rec_done0"), sem("rec_done1")]
        xr_ready = sem("xr_ready")
        ln2_chain = sem("ln2_chain")
        rs2_chain = sem("rs2_chain")
        x2n_ready = sem("x2n_ready")
        route = sem("route")
        seen_ready = sem("seen_ready")
        tok_chain = sem("tok_chain")
        le_ready = sem("le_ready")
        rows_ready = sem("rows_ready")
        passed = sem("passed")
        bias_ready = sem("bias_ready")
        we_T = sem("we_T")
        weT_ready = sem("weT_ready")
        gn_ready = sem("gn_ready")
        gT_made = sem("gT_made")
        gT_ready = sem("gT_ready")
        y_made = sem("y_made")
        y_chain = sem("y_chain")

        WEIGHT = {"K": 0, "Q": 1, "V": 2, "O": 3}
        PARTS = [(0, 0), (0, 1), (1, 0)]
        ROUTE1, ROUTE2 = 7, 6
        ROUTE = ROUTE1 + ROUTE2
        STACK_DMAS = 2 * len(PAIRS) + 2
        STAGE = {"XT": 3, "CT": 3, "K": 3, "Q": 3, "V": 1, "MTa": 1, "MTb": 0, "C1T": 0,
                 "C2T": -1, "NT": -1, "O": -1, "X2T": -1, "R": -1, "L": -1}
        FULL = range(1, B - 3)
        assert len(FULL) % RING == 0

        def g_bank(e, r):
            return ((P2[0], P2[1]), (CB, M[0]))[e % 2][r]

        def we_bank(e):
            return (P1[0], P1[1], P2[0], P2[1])[e % 4]

        def bank_of(task):
            return M[BANK[task]]

        def has(stage, i, known):
            return True if known is None else 0 <= known + stage < B

        def wait(eng, s, value):
            if isinstance(value, int) and value <= 0:
                return
            eng.wait_ge(s, value)

        def apart(eng):
            eng.sem_inc(passed, 1)

        def claim(pe, task, i, known):
            order = [t for t in TASKS if BANK[t] == BANK[task]]
            n = order.index(task)
            back = 0
            while True:
                n -= 1
                if n < 0:
                    n, back = len(order) - 1, back + 1
                if known is not None and known - back < -3:
                    return
                t = order[n]
                if known is None and back and STAGE[t] < 0:
                    return
                if has(STAGE[t], i, None if known is None else known - back):
                    wait(pe, took[t], i - back + STAGE[t] + 1)
                    return

        def slot_of(slot, stage):
            return (slot + stage) % RING

        block = es.enter_context(nc.Block())

        def looped(eng, turn):
            for i in range(-3, FULL[0]):
                turn(i, i, i % RING, lambda st, i=i: (i + st) // RING + 1)
            with eng.Fori(0, len(FULL) // RING) as j:
                for u in range(RING):
                    c = u + FULL[0]
                    turn(j * RING + c, None, c % RING, lambda st, c=c: j + ((c + st) // RING + 1))
            for i in range(FULL[-1] + 1, B + 1):
                turn(i, i, i % RING, lambda st, i=i: (i + st) // RING + 1)

        @block.sync
        def _(sp):
            for b in range(RING):
                sp.dma_start(x_sb[:, b], x_v[b]).then_inc(x_landed[b], 16)
                sp.dma_start(c_sb[:, b], c_v[b]).then_inc(c_landed[b], 16)
            sp.dma_start(mask_i[:, :], mask.rearrange("b o u s -> (b o u) s")).then_inc(mask_landed, 16)
            for n, w in (("V", wv), ("O", wo)):
                sp.dma_start(w_raw[:, WEIGHT[n]], w.rearrange("(c p) n -> p c n", p=P)).then_inc(w_landed, 16)
            sp.dma_start(wg_sb[:, :, :], wg.rearrange("(c p) e -> p c e", p=P)).then_inc(w_landed, 16)
            sp.dma_start(bv_sb[:, :], bv.rearrange("(c p) -> p c", p=P), allow_slow_non_contiguous=True).then_inc(w_landed, 16)
            sp.dma_start(bo_sb[:, :], bo.rearrange("(o n) -> o n", o=1).to_broadcast([P, D])).then_inc(w_landed, 16)
            sp.dma_start(be_sb[:, :, :], b_exp.rearrange("(o e) d -> o e d", o=1).to_broadcast([P, E, D])).then_inc(we_landed, 16)
            sp.wait_ge(dve_const, 2)
            for s in range(RING):
                sp.dma_start(negmax_d[s, 0:3], zero_row[:, :].rearrange("r (o t) -> r o t", o=1).to_broadcast([3, H, S])
                             ).then_inc(const_out, 16)
                sp.dma_start(ks[XROW:KROWS, s], ones_row[:, :].rearrange("r (o t) -> r o t", o=1).to_broadcast([3, H, S])
                             ).then_inc(const_out, 16)
            sp.wait_ge(dve_const, 7)
            sp.dma_start(maskp_d, mask_p[:, :, :]).then_inc(maskp_out, 16)
            sp.wait_ge(maskp_out, 16)

            def negmax_rows(half, b, s, rnd_b):
                hs = slice(half * HH, (half + 1) * HH)
                wait(sp, nm_chain[half], 2 * (b + 1))
                apart(sp)
                sp.dma_start(negmax_d[s, 3:6, hs].rearrange("r h t -> h r t"), nmp[:, half]).then_inc(nm_out[half], 16)
                wait(sp, nm_out[half], 16 * (b + 1))
                apart(sp)
                sp.dma_start(qs[MROW:KROWS, s, hs].rearrange("r h t -> r (h t)"),
                             negmax_d[s, :, hs].rearrange("r h t -> r (h t)")).then_inc(nm_landed[half][s], 16)

            def turn(i, known, slot, rnd):
                if has(3, i, known) and not (known is not None and known + 3 < RING):
                    s = slot_of(slot, 3)
                    wait(sp, xn_ready, i + 1)
                    apart(sp)
                    sp.dma_start(x_sb[:, s], x_v[i + 3]).then_inc(x_landed[s], 16)
                    wait(sp, made["CT"], i + 1)
                    apart(sp)
                    sp.dma_start(c_sb[:, s], c_v[i + 3]).then_inc(c_landed[s], 16)
                if has(-1, i, known):
                    s = slot_of(slot, -1)
                    wait(sp, max_done, H * i)
                    apart(sp)
                    sp.dma_start(xr[:, s], x_v[i - 1]).then_inc(xr_landed[s], 16)
                if has(1, i, known):
                    s = slot_of(slot, 1)
                    wait(sp, max_done, H * i)
                    apart(sp)
                    sp.dma_start(mask_c[:, s], m_v[i + 1], allow_slow_non_contiguous=True).then_inc(mc_landed[s], 16)

                def parts_out(side):
                    s = slot_of(slot, 2)
                    wait(sp, split_done, 2 * (i + 3) - side)
                    apart(sp)
                    sp.dma_start(split_d[s, side].rearrange("r (c p) t -> p (r c) t", p=P),
                                 parts[:, side].rearrange("p r c t -> p (r c) t")).then_inc(split_out[side][s], 16)

                def parts_back(side, stack):
                    s = slot_of(slot, 2)
                    wait(sp, split_out[side][s], 16 * rnd(2))
                    apart(sp)
                    src = split_d[s, side].rearrange("r (h d) t -> r d h t", d=DEP)
                    for n, pair in enumerate(PAIRS):
                        sp.dma_start(stack[n * DEP:(n + 1) * DEP, s], src[pair[side]]).then_inc(stack_landed[s], 16)

                if has(2, i, known):
                    s = slot_of(slot, 2)
                    wait(sp, stack_landed[s], 16 * STACK_DMAS * (rnd(2) - 1))
                    apart(sp)
                    parts_out(1)
                    if known is not None and known < 0:
                        parts_back(1, ks)
                    parts_out(0)
                if has(0, i, known):
                    negmax_rows(1, i, slot, rnd(0))
                if has(2, i, known):
                    s = slot_of(slot, 2)
                    wait(sp, p2_ready, H * i)
                    apart(sp)
                    sp.dma_start(qs[MROW:MROW + 3, s].rearrange("r h t -> r (h t)"),
                                 ks[XROW:KROWS, s].rearrange("r h t -> r (h t)")).then_inc(stack_landed[s], 16)
                    sp.dma_start(ks[MROW:MROW + 3, s], maskp_d[i + 2].rearrange("r (o t) -> r o t", o=1).to_broadcast([3, H, S])
                                 ).then_inc(stack_landed[s], 16)
                    if known is None or known >= 0:
                        parts_back(1, ks)
                    parts_back(0, qs)
                if known == B - 1:
                    sp.wait_ge(p2_ready, H * (B - 1))
                    sp.dma_start(w_in[:, :, :, :], w_exp.rearrange("e (c p) h -> p e c h", p=P)).then_inc(we_landed, 16)
                if has(1, i, known):
                    negmax_rows(0, i + 1, slot_of(slot, 1), rnd(1))
                if has(-1, i, known):
                    s = slot_of(slot, -1)
                    wait(sp, took["O"], i)
                    apart(sp)
                    sp.dma_start(out_v[i - 1], rows[:, s, :, 0:D]).then_inc(store_out[s], 16)

            looped(sp, turn)

            for s in range(RING):
                n = len(range(s, B, RING))
                sp.wait_ge(scat_out[s], 32 * (n + 1))
            sp.wait_ge(took["O"], B)
            slots_v = slots_d.rearrange("(e g p) c -> e p g c", e=E, p=P)
            for e in range(E):
                if e >= GR:
                    sp.wait_ge(y_chain, 4 * (e - GR + 1))
                sp.dma_start(g_rows[:, e % GR], slots_v[e]).then_inc(g_landed[e], 16)
            for s in range(2):
                sp.wait_ge(y_out[s], 16 * GT * (E // 2))

        @block.gpsimd
        def _(pool):
            g = nc.gpsimd
            for s in range(RING):
                pool.sem_inc(store_out[s], 16)
            g.memset(far, FAR).then_inc(pool_const, 1)
            g.memset(expo[:, :], -0.5).then_inc(pool_const, 1)
            g.memset(batch_step[:, :], float(S)).then_inc(pool_const, 1)
            g.memset(ident[:, :], 0.0).then_inc(pool_const, 1)
            g.memset(tri[:, :], 1.0).then_inc(pool_const, 1)
            pool.wait_ge(pool_const, 5)
            g.affine_select(out=ident[:, :], in_=ident[:, :], compare_op=ALU.not_equal, fill=1.0,
                            base=0, pattern=[[-1, P]], channel_multiplier=1).then_inc(pool_const, 1)
            g.affine_select(out=tri[:, :], in_=tri[:, :], compare_op=ALU.is_gt, fill=0.0,
                            base=0, pattern=[[1, P]], channel_multiplier=-1).then_inc(pool_const, 1)
            g.iota(iota8[:, :, :], pattern=[[0, TC], [1, E]], base=0, channel_multiplier=0,
                   allow_small_or_imprecise_dtypes=True).then_inc(pool_const, 1)
            g.iota(tokf[:, :], pattern=[[P, TC]], base=-S, channel_multiplier=1,
                   allow_small_or_imprecise_dtypes=True).then_inc(pool_const, 1)

            def negmax_parts(half, b):
                c = nm_chain[half]
                pool.wait_ge(took["MTb" if half else "MTa"], b + 1)
                apart(pool)
                g.tensor_tensor(nmp[:, half, 1], nm[:, half], zeros[0:HH, 0:S], ALU.add).then_inc(c, 1)
                pool.wait_ge(c, 2 * b + 1)
                apart(pool)
                g.tensor_tensor(nmp[:, half, 2], nm[:, half], nmp[:, half, 1], ALU.subtract).then_inc(c, 1)

            def xnT_low(b):
                pool.wait_ge(high["XT"], b + 1)
                apart(pool)
                g.tensor_tensor(xnT[:, 1], xnT_full[:, :, :], xnT[:, 0].bitcast(F32), ALU.subtract).then_inc(xnT_ready, 1)

            def rest_part(task, b):
                side = 1 if task == "K" else 0
                pool.wait_ge(high_done[task], b + 1)
                apart(pool)
                g.tensor_tensor(qk[:, side], qk[:, side], parts[:, side, 0], ALU.subtract).then_inc(rest_done[task], 1)

            def low_part(task, b):
                side = 1 if task == "K" else 0
                pool.wait_ge(mid_done[task], b + 1)
                apart(pool)
                g.tensor_tensor(parts[:, side, 2], qk[:, side], parts[:, side, 1], ALU.subtract).then_inc(split_done, 1)

            def turn(i, known, slot, rnd):
                if has(0, i, known):
                    negmax_parts(1, i)
                if has(3, i, known):
                    pool.wait_ge(ln1_chain, 4 * (i + 4))
                    apart(pool)
                    g.tensor_scalar(rs1[:, 0], mv1[:, :, 1], EPS, None, ALU.add).then_inc(rs1_chain, 1)
                    pool.wait_ge(rs1_chain, 2 * (i + 3) + 1)
                    apart(pool)
                    g.tensor_tensor(rs1[:, 1], rs1[:, 0], expo[:, :], ALU.pow).then_inc(rs1_chain, 1)
                if known in (-3, -2):
                    far_v = slots_d.rearrange("(n p r) c -> n p (r c)", p=P, r=FARR)
                    half = FARS // 2 * (known + 3)
                    for n in range(half, half + FARS // 2):
                        g.dma_start(far_v[n], far).then_inc(scat_out[n // 2] if n < 2 * RING else far_out, 16)
                if has(-1, i, known):
                    s = slot_of(slot, -1)
                    pool.wait_ge(xr_landed[s], 16 * rnd(-1))
                    apart(pool)
                    g.tensor_tensor(xr[:, s], xr[:, s], bo_sb[:, :].rearrange("p (o n) -> p o n", o=1).to_broadcast([P, TC, D]),
                                    ALU.add).then_inc(xr_ready, 1)
                if has(3, i, known):
                    xnT_low(i + 3)
                    rest_part("K", i + 3)
                if has(-1, i, known):
                    s = slot_of(slot, -1)
                    pool.wait_ge(ln2_chain, 4 * i)
                    apart(pool)
                    g.tensor_scalar(rs2[:, :], mv2[:, :, 1], EPS, None, ALU.add).then_inc(rs2_chain, 1)
                    pool.wait_ge(rs2_chain, 3 * (i - 1) + 1)
                    apart(pool)
                    g.tensor_tensor(rows[:, s, :, RSTD], rs2[:, :], expo[:, :], ALU.pow).then_inc(rs2_chain, 1)
                    g.tensor_copy(rows[:, s, :, MEAN], mv2[:, :, 0]).then_inc(rs2_chain, 1)
                if has(-1, i, known):
                    s = slot_of(slot, -1)
                    g.tensor_tensor(tokf[:, :], tokf[:, :], batch_step[:, :], ALU.add).then_inc(tok_chain, 1)
                    pool.wait_ge(tok_chain, 2 * (i - 1) + 1)
                    apart(pool)
                    g.tensor_copy(rows[:, s, :, TOK], tokf[:, :]).then_inc(tok_chain, 1)
                if has(1, i, known):
                    negmax_parts(0, i + 1)
                if has(3, i, known):
                    low_part("K", i + 3)
                if has(3, i, known):
                    rest_part("Q", i + 3)
                    low_part("Q", i + 3)
                if has(-1, i, known):
                    pool.wait_ge(made["L"], i)
                    apart(pool)
                    for t in range(TC):
                        if t:
                            pool.wait_ge(seen_ready, TC * i + t)
                            apart(pool)
                        g.tensor_tensor(seen[:, :], seen[:, :], oh[:, t], ALU.add).then_inc(seen_ready, 1)
                if has(-1, i, known):
                    s = slot_of(slot, -1)
                    pool.wait_ge(rows_ready, i)
                    apart(pool)
                    for t in range(TC):
                        g.indirect_dma_start(slots_d, bass.IndirectOffsetOnAxis(ap=sloti[:, s, t:t + 1], axis=0),
                                             rows[:, s, t, :], None, bounds_check=T - 1, oob_is_err=False
                                             ).then_inc(scat_out[s], 16)
                if known == 0:
                    pool.wait_ge(bias_ready, 3)
                    pool.wait_ge(far_out, 16 * (FARS - 2 * RING))
                    for n in range(RING):
                        pool.wait_ge(scat_out[n], 32)

            looped(pool, turn)

            for s in range(RING):
                pool.wait_ge(store_out[s], 16 * (len(range(s, B, RING)) + 1))
            for e in range(E):
                for t in range(GT):
                    if t % 2 == 0:
                        pool.wait_ge(y_chain, 4 * e + 2 * (t // 2 + 1))
                    g.indirect_dma_start(out_rows, bass.IndirectOffsetOnAxis(ap=g_tok[:, e, t:t + 1], axis=0),
                                         g_out[:, e % 2, t, :], None, bounds_check=T - 1, oob_is_err=False
                                         ).then_inc(y_out[e % 2], 16)

        @block.scalar
        def _(act):
            a = nc.scalar

            def evac(task, b, dst):
                act.wait_ge(made[task], b + 1)
                a.activation(dst.rearrange("p c t -> p (c t)"), bank_of(task)[:, :], ACT.Copy
                             ).then_inc(high[task] if task in ("CT", "NT") else took[task], 1)

            def weight_high(n):
                a.activation(w_part[:, n, 0], w_raw[:, n], ACT.Copy).then_inc(w_high, 1)

            def projected(task, b):
                side = 1 if task == "K" else 0
                act.wait_ge(made[task], b + 1)
                wait(act, split_done, 2 * b)
                for c in range(KC):
                    r = a.activation(qk[:, side, c], bank_of(task)[:, c * S:(c + 1) * S], ACT.Identity,
                                     bias=bias_qk[:, side, c:c + 1])
                r.then_inc(took[task], 1)

            def high_part(task, b, known, slot, rnd):
                side = 1 if task == "K" else 0
                act.wait_ge(took[task], b + 1)
                if has(2, None, known):
                    act.wait_ge(split_out[side][slot_of(slot, 2)], 16 * rnd(2))
                a.activation(parts[:, side, 0], qk[:, side], ACT.Copy).then_inc(high_done[task], 1)

            def mid_part(task, b):
                side = 1 if task == "K" else 0
                act.wait_ge(rest_done[task], b + 1)
                a.activation(parts[:, side, 1], qk[:, side], ACT.Copy).then_inc(mid_done[task], 1)

            def neg_evac(task, half, b):
                act.wait_ge(made[task], b + 1)
                wait(act, nm_out[half], 16 * b)
                a.activation(nmp[:, half, 0], bank_of(task)[0:HH, 0:S], ACT.Copy, scale=-1.0).then_inc(nm_high[half], 1)

            def sums_evac(half, b, quads):
                act.wait_ge(pv_done, quads)
                wait(act, made["C1T"], b + half)
                a.activation(av[:, half], CB[:, :].rearrange("p (g t) -> p g t", g=2), ACT.Copy).then_inc(av_ready[half], 1)

            def weights(e):
                act.wait_ge(we_T, e + 1)
                a.activation(weT[:, e].rearrange("p c f -> p (c f)"), we_bank(e)[:, :], ACT.Copy).then_inc(weT_ready, 1)

            for n, w in (("K", wk), ("Q", wq)):
                act.dma_start(w_raw[:, WEIGHT[n]], w.rearrange("(c p) n -> p c n", p=P)).then_inc(wqk_landed[WEIGHT[n]], 16)
            for n, v in enumerate((bq, bk)):
                act.dma_start(bias_qk[:, n, :], v.rearrange("(c p) -> p c", p=P),
                              allow_slow_non_contiguous=True).then_inc(bqk_landed, 16)

            def turn(i, known, slot, rnd):
                def probabilities(n):
                    act.wait_ge(p2_ready, H * i + (n + 1))
                    wait(act, pv_done, QUADS * i + (n // 2 - 1))
                    a.activation(probs[:, n % 4], P2[n % 2][:, :], ACT.Exp,
                                 bias=mbias[:, slot, (n // 2) % 2:(n // 2) % 2 + 1], scale=SCALE).then_inc(exp_done, 1)

                for k in range(QUADS):
                    if k == 1 and has(3, i, known):
                        wait(act, made["V"], i + 1)
                        evac("CT", i + 3, cT[:, slot_of(slot, 3), 0])
                    if k == 5 and has(0, i, known):
                        sums_evac(0, i, QUADS * i + QUADS // 2)
                    if k == 5 and has(3, i, known):
                        projected("Q", i + 3)
                    if has(0, i, known):
                        if k == 0:
                            act.wait_ge(mbias_ready, i + 1)
                        probabilities(2 * k)
                    if k == 0 and has(0, i, known):
                        neg_evac("MTb", 1, i)
                    if has(0, i, known):
                        probabilities(2 * k + 1)
                    if k == 0 and has(-1, i, known):
                        sums_evac(1, i - 1, QUADS * i)
                    if k == 5 and has(-1, i, known):
                        evac("X2T", i - 1, x2T[:, :, :])
                    if k == 5 and has(3, i, known):
                        high_part("Q", i + 3, known, slot, rnd)
                    if known == B:
                        weights(k)
                    if k == 1 and known == -2:
                        act.wait_ge(w_landed, 16 * 5)
                        weight_high(WEIGHT["V"])
                        weight_high(WEIGHT["O"])
                    if k == 1 and has(3, i, known):
                        projected("K", i + 3)
                    if k == 1 and has(-1, i, known):
                        evac("NT", i - 1, anT[:, 0])
                    if k == 2 and has(3, i, known):
                        high_part("K", i + 3, known, slot, rnd)
                        evac("XT", i + 3, xnT_full)
                        act.wait_ge(took["XT"], i + 4)
                        a.activation(xnT[:, 0], xnT_full[:, :, :], ACT.Copy).then_inc(high["XT"], 1)
                    if k == 4 and has(1, i, known):
                        neg_evac("MTa", 0, i + 1)
                    if k == 4 and has(3, i, known):
                        mid_part("K", i + 3)
                    if k == 6 and has(3, i, known):
                        mid_part("Q", i + 3)
                    if k == 7 and has(1, i, known):
                        s = slot_of(slot, 1)
                        wait(act, pv_done, QUADS * i)
                        act.wait_ge(made["V"], i + 2)
                        a.activation(v_sb[:, s, :, :, 0:DEP],
                                     bank_of("V")[:, :].rearrange("p (c h d) -> p c h d", c=TC, d=DEP),
                                     ACT.Copy).then_inc(took["V"], 1)
                    if k == 7 and has(-1, i, known):
                        act.wait_ge(route, ROUTE * (i - 1) + ROUTE1)
                        a.activation(le[:, :, :], ld[:, :, :], ACT.Exp).then_inc(le_ready, 1)

            for n in "KQ":
                act.wait_ge(wqk_landed[WEIGHT[n]], 16)
                weight_high(WEIGHT[n])
            act.wait_ge(bqk_landed, 16 * 2)
            looped(act, turn)

            for e in range(E):
                for r in range(2):
                    act.wait_ge(gT_made, 2 * e + r + 1)
                    if e >= 2:
                        act.wait_ge(y_made, 2 * (e - 2) + r + 1)
                    a.activation(g_T[:, e % 2, r].rearrange("p c t -> p (c t)"), P1[r][:, :], ACT.Copy).then_inc(gT_ready, 1)

        @block.vector
        def _(dve):
            v = nc.vector

            def weight_low(n):
                dve.wait_ge(w_high, n + 1)
                v.tensor_tensor(w_part[:, n, 1], w_raw[:, n], w_part[:, n, 0].bitcast(F32), ALU.subtract).then_inc(w_low, 1)

            def low_part(task, b, parts_of):
                dve.wait_ge(high[task], b + 1)
                v.tensor_tensor(parts_of[:, 1], bank_of(task)[:, :].rearrange("p (c t) -> p c t", c=KC),
                                parts_of[:, 0].bitcast(F32), ALU.subtract).then_inc(took[task], 1)

            def constants():
                dve.wait_ge(mask_landed, 16)
                v.tensor_scalar(mask_f[:, :], mask_i[:, :], NEG / SCALE, None, ALU.mult).then_inc(dve_const, 1)
                dve.wait_ge(dve_const, 3)
                v.tensor_copy(mask_p[:, 0], mask_f[:, :]).then_inc(dve_const, 1)
                dve.wait_ge(dve_const, 4)
                v.tensor_tensor(mask_f[:, :], mask_f[:, :], mask_p[:, 0], ALU.subtract).then_inc(dve_const, 1)
                dve.wait_ge(dve_const, 5)
                v.tensor_copy(mask_p[:, 1], mask_f[:, :]).then_inc(dve_const, 1)
                dve.wait_ge(dve_const, 6)
                v.tensor_tensor(mask_p[:, 2], mask_f[:, :], mask_p[:, 1], ALU.subtract).then_inc(dve_const, 1)

            def normalise(task, half, b):
                src = bank_of(task)[:, :].rearrange("p (q h e) -> p q h e", q=TC, e=32)
                dve.wait_ge(made[task], b + 1)
                v.reciprocal(rec[:, half], src[:, :, :, DEP]).then_inc(rec_done[half], 1)
                dve.wait_ge(rec_done[half], b + 1)
                if half == 0:
                    wait(dve, made["NT"], b)
                v.tensor_tensor(an[:, :, half * P:(half + 1) * P].rearrange("p q (h d) -> p q h d", d=DEP),
                                src[:, :, :, 0:DEP],
                                rec[:, half].rearrange("p q (h o) -> p q h o", o=1).to_broadcast([P, TC, HH, DEP]),
                                ALU.mult).then_inc(took[task], 1)

            def neg_rest(task, half, b):
                dve.wait_ge(nm_high[half], b + 1)
                wait(dve, nm_chain[half], 2 * b)
                v.scalar_tensor_tensor(out=nm[:, half], in0=bank_of(task)[0:HH, 0:S], scalar=-1.0,
                                       in1=nmp[:, half, 0], op0=ALU.mult, op1=ALU.subtract).then_inc(took[task], 1)

            def statistics(src, st, mv, chain, b):
                for t in range(TC):
                    v.bn_stats(st[:, t], src[:, t]).then_inc(chain, 1)
                for t in range(TC):
                    dve.wait_ge(chain, 4 * b + t + 1)
                    apart(dve)
                    v.bn_aggr(mv[:, t], st[:, t]).then_inc(chain, 1)

            def turn(i, known, slot, rnd):
                sp1 = slot_of(slot, -1)

                def maximum(h):
                    dve.wait_ge(p1_ready, H * (i + 1) + (h + 1))
                    if h == 0:
                        wait(dve, made["MTa"], i + 1)
                    if h == HH:
                        wait(dve, made["MTb"], i + 1)
                    v.tensor_reduce(mx[:, h], P1[h % 2][:, :].rearrange("p (q t) -> p q t", q=TC),
                                    AX.X, ALU.max).then_inc(max_done, 1)

                def stepped(n):
                    dve.wait_ge(route, ROUTE * (i - 1) + n)

                def top_logit():
                    dve.wait_ge(made["R"], i)
                    v.tensor_copy(lg[:, :, :], bank_of("R")[:, 0:TC * E].rearrange("p (q e) -> p q e", e=E)
                                  ).then_inc(took["R"], 1)
                    dve.wait_ge(took["R"], i)
                    apart(dve)
                    for t in range(TC):
                        v.max(top[:, t], lg[:, t]).then_inc(route, 1)

                def top_expert():
                    stepped(2)
                    apart(dve)
                    for t in range(TC):
                        v.max_index(topi[:, t], top[:, t], lg[:, t]).then_inc(route, 1)
                    v.tensor_tensor(ld[:, :, :], lg[:, :, :], top[:, :, 0:1].to_broadcast([P, TC, E]), ALU.subtract).then_inc(route, 1)

                def one_hot():
                    stepped(5)
                    v.tensor_copy(expf[:, :], topi[:, :, 0]).then_inc(route, 1)
                    stepped(6)
                    dve.wait_ge(seen_ready, TC * i)
                    v.tensor_tensor(oh[:, :, :], iota8[:, :, :],
                                    expf[:, :].rearrange("p (q o) -> p q o", o=1).to_broadcast([P, TC, E]), ALU.is_equal
                                    ).then_inc(route, 1)

                def location():
                    dve.wait_ge(made["L"], i)
                    v.tensor_tensor(loc[:, :, :], bank_of("L")[:, 0:TC * E].rearrange("p (q e) -> p q e", e=E),
                                    oh[:, :, :], ALU.mult).then_inc(took["L"], 1)
                    dve.wait_ge(took["L"], i)
                    v.tensor_reduce(locv[:, :], loc[:, :, :], AX.X, ALU.add).then_inc(route, 1)
                    dve.wait_ge(le_ready, i)
                    v.tensor_reduce(lsum[:, :], le[:, :, :], AX.X, ALU.add).then_inc(route, 1)

                def slot_and_gate():
                    stepped(ROUTE1 + 2)
                    v.tensor_scalar(late[:, :], locv[:, :], float(CAP), FAR, ALU.is_ge, ALU.mult).then_inc(route, 1)
                    v.scalar_tensor_tensor(out=slotf[:, :], in0=expf[:, :], scalar=float(CAP), in1=locv[:, :],
                                           op0=ALU.mult, op1=ALU.add).then_inc(route, 1)
                    v.reciprocal(rows[:, sp1, :, GATE], lsum[:, :]).then_inc(route, 1)
                    stepped(ROUTE1 + 5)
                    v.tensor_tensor(slotf[:, :], slotf[:, :], late[:, :], ALU.add).then_inc(route, 1)
                    stepped(ROUTE)
                    v.tensor_copy(sloti[:, sp1], slotf[:, :]).then_inc(rows_ready, 1)

                for k in range(QUADS):
                    if k == 1 and has(0, i, known):
                        neg_rest("MTb", 1, i)
                    if k == 1 and has(3, i, known):
                        low_part("CT", i + 3, cT[:, slot_of(slot, 3)])
                    if k == 2 and has(3, i, known):
                        dve.wait_ge(rs1_chain, 2 * (i + 4))
                        wait(dve, made["XT"], i + 3)
                        for t in range(TC):
                            r = v.tensor_scalar(xn[:, t], x_sb[:, slot_of(slot, 3), t], mv1[:, t, 0:1],
                                                rs1[:, 1, t:t + 1], ALU.subtract, ALU.mult)
                        r.then_inc(xn_ready, 1)
                    if k == 5 and has(-1, i, known):
                        dve.wait_ge(rs2_chain, 3 * i)
                        for t in range(TC):
                            r = v.tensor_scalar(x2n[:, t], rows[:, sp1, t, 0:D], rows[:, sp1, t, MEAN:MEAN + 1],
                                                rows[:, sp1, t, RSTD:RSTD + 1], ALU.subtract, ALU.mult)
                        r.then_inc(x2n_ready, 1)
                    if k == 7 and has(-1, i, known):
                        one_hot()
                    if has(1, i, known):
                        maximum(2 * k)
                    if k == 1 and has(3, i, known):
                        dve.wait_ge(x_landed[slot_of(slot, 3)], 16 * rnd(3))
                        statistics(x_sb[:, slot_of(slot, 3)], st1, mv1, ln1_chain, i + 3)
                    if k == 1 and has(-1, i, known):
                        normalise("C2T", 1, i - 1)
                    if k == 2 and has(-1, i, known):
                        low_part("NT", i - 1, anT)
                    if k == 3 and has(-1, i, known):
                        dve.wait_ge(made["O"], i)
                        dve.wait_ge(xr_ready, i)
                        dve.wait_ge(store_out[sp1], 16 * rnd(-1))
                        dve.wait_ge(scat_out[sp1], 32 * rnd(-1))
                        v.tensor_tensor(rows[:, sp1, :, 0:D], bank_of("O")[:, :].rearrange("p (q n) -> p q n", q=TC),
                                        xr[:, sp1], ALU.add).then_inc(took["O"], 1)
                    if has(1, i, known):
                        maximum(2 * k + 1)
                    if k == 2 and has(1, i, known):
                        s = slot_of(slot, 1)
                        dve.wait_ge(mc_landed[s], 16 * rnd(1))
                        wait(dve, exp_done, H * i)
                        v.tensor_scalar(mbias[:, s], mask_c[:, s], NEG, None, ALU.mult).then_inc(mbias_ready, 1)
                    if k == 2 and known == -2:
                        dve.wait_ge(w_landed, 16 * 5)
                        v.tensor_copy(bv_wide[:, :, :], bv_sb[:, :].rearrange("p (c o) -> p c o", o=1).to_broadcast([P, KC, P])
                                      ).then_inc(bias_ready, 1)
                        weight_low(WEIGHT["V"])
                        weight_low(WEIGHT["O"])
                    if k == 3 and has(-1, i, known):
                        dve.wait_ge(took["O"], i)
                        statistics(rows[:, sp1, :, 0:D], st2, mv2, ln2_chain, i - 1)
                    if k == 4 and has(1, i, known):
                        neg_rest("MTa", 0, i + 1)
                    if k == 6 and has(0, i, known):
                        normalise("C1T", 0, i)
                    if k == 6 and has(-1, i, known):
                        top_logit()
                        top_expert()
                    if k == 7 and has(-1, i, known):
                        location()
                        slot_and_gate()
                if known == -3:
                    constants()
                if known == -1:
                    dve.wait_ge(bias_ready, 2)
                    v.tensor_tensor(bo_sb[:, :], bo_sb[:, :], bank_of("O")[:, 0:D], ALU.add).then_inc(bias_ready, 1)

            v.memset(ones_row[:, :], 1.0).then_inc(dve_const, 1)
            v.memset(zero_row[:, :], 0.0).then_inc(dve_const, 1)
            v.memset(onesm[:, :], 1.0)
            v.memset(zeros[:, :], 0.0)
            v.memset(seen[:, :], 0.0).then_inc(seen_ready, TC)
            for s in range(RING):
                v.memset(v_sb[:, s], 1.0)
            weight_low(WEIGHT["K"])
            weight_low(WEIGHT["Q"])
            looped(dve, turn)

            dve.wait_ge(we_landed, 32)

            def slots_normed(e):
                dve.wait_ge(g_landed[e], 16)
                if e >= 2:
                    dve.wait_ge(gT_made, 2 * (e - 1))
                for t in range(GT):
                    v.tensor_scalar(g_n[:, e % 2, t], g_rows[:, e % GR, t, 0:D], g_rows[:, e % GR, t, MEAN:MEAN + 1],
                                    g_rows[:, e % GR, t, RSTD:RSTD + 1], ALU.subtract, ALU.mult).then_inc(gn_ready, 1)

            slots_normed(0)
            slots_normed(1)
            for e in range(E):
                if e + 2 < E:
                    slots_normed(e + 2)
                if e >= 2:
                    dve.wait_ge(y_out[e % 2], 16 * GT * (e // 2))
                v.tensor_copy(g_tok[:, e], g_rows[:, e % GR, :, TOK])
                for r in range(2):
                    dve.wait_ge(y_made, 2 * e + r + 1)
                    if 2 * e + r:
                        dve.wait_ge(y_chain, 4 * e + 2 * r)
                    v.tensor_tensor(g_y[:, :, :], g_bank(e, r)[:, :].rearrange("p (q n) -> p q n", q=2),
                                    be_sb[:, e].rearrange("p (o n) -> p o n", o=1).to_broadcast([P, 2, D]),
                                    ALU.add).then_inc(y_chain, 1)
                    dve.wait_ge(y_chain, 4 * e + 2 * r + 1)
                    for q in range(2):
                        t = 2 * r + q
                        o = v.scalar_tensor_tensor(out=g_out[:, e % 2, t], in0=g_y[:, q], scalar=g_rows[:, e % GR, t, GATE:GATE + 1],
                                                   in1=g_rows[:, e % GR, t, 0:D], op0=ALU.mult, op1=ALU.add)
                    o.then_inc(y_chain, 1)

        @block.tensor
        def _(pe):
            t_ = nc.tensor
            pe.wait_ge(pool_const, 9)

            def transposes(task, src):
                o = bank_of(task)
                for c in range(2):
                    for t in range(2):
                        r = t_.transpose(o[:, c * S + t * P:c * S + (t + 1) * P], src(c, t), ident[:, :])
                r.then_inc(made[task], 1)

            def product(task, lhs, rhs):
                o = bank_of(task)
                for n in range(2):
                    for c in range(KC):
                        for u, (lp, rp) in enumerate(PARTS):
                            r = t_.matmul(o[:, n * S:(n + 1) * S], lhs(lp, c, n), rhs(rp, c, n),
                                          start=(c == 0 and u == 0), stop=(c == KC - 1 and u == len(PARTS) - 1))
                r.then_inc(made[task], 1)

            def times_v(i, known, k, slot):
                g, c = k // 2, k % 2
                pe.wait_ge(exp_done, H * i + (2 * k + 2))
                if k == 0:
                    pe.wait_ge(took["V"], i + 1)
                    wait(pe, av_ready[1], i)
                if k == QUADS // 2:
                    pe.wait_ge(av_ready[0], i + 1)
                for j in range(4):
                    n = 2 * k + j // 2
                    r = t_.matmul(CB[32 * j:32 * j + 32, (g % 2) * S:(g % 2 + 1) * S], v_sb[:, slot, c, 4 * g + j, :],
                                  probs[:, n % 4, (j % 2) * S:(j % 2 + 1) * S], start=(c == 0), stop=(c == 1))
                r.then_inc(pv_done, 1)

            def negmax(task, half, b, i, known):
                pe.wait_ge(max_done, H * b + HH * (half + 1))
                claim(pe, task, i, known)
                for q in range(TC):
                    r = t_.transpose(bank_of(task)[0:HH, q * P:(q + 1) * P], mx[:, half * HH:(half + 1) * HH, q], ident[:, :])
                r.then_inc(made[task], 1)

            def turn(i, known, slot, rnd):
                if known == -1:
                    pe.wait_ge(w_low, 4)
                    pe.wait_ge(bias_ready, 1)
                    for c in range(KC):
                        r = t_.matmul(bank_of("O")[:, 0:D], bv_wide[:, c, :], w_raw[:, WEIGHT["O"], c, :], start=(c == 0), stop=(c == KC - 1))
                    r.then_inc(bias_ready, 1)
                    pe.wait_ge(const_out, 16 * 2 * RING)

                def logits_by_key(n):
                    k = n // 2
                    if n == 0:
                        pe.wait_ge(nm_landed[0][slot], 16 * rnd(0))
                    if n == QUADS:
                        pe.wait_ge(nm_landed[1][slot], 16 * rnd(0))
                    wait(pe, exp_done, H * i + (n - 1))
                    for j in range(2):
                        h, c = 4 * (k // 2) + 2 * (n % 2) + j, k % 2
                        r = t_.matmul(P2[n % 2][:, j * S:(j + 1) * S], ks[0:KROWS, slot, h, c * P:(c + 1) * P],
                                      qs[0:KROWS, slot, h, :], start=True, stop=True)
                    r.then_inc(p2_ready, 1)

                def logits_by_query(h):
                    s = slot_of(slot, 1)
                    if h == 0:
                        pe.wait_ge(stack_landed[s], 16 * STACK_DMAS * rnd(1))
                    wait(pe, max_done, H * (i + 1) + (h - 1))
                    for q in range(TC):
                        r = t_.matmul(P1[h % 2][:, q * S:(q + 1) * S], qs[0:XROW, s, h, q * P:(q + 1) * P],
                                      ks[0:XROW, s, h, :], start=True, stop=True)
                    r.then_inc(p1_ready, 1)

                s1, s3 = slot_of(slot, 1), slot_of(slot, 3)
                for k in range(QUADS):
                    if k == 3 and has(3, i, known):
                        pe.wait_ge(xn_ready, i + 4)
                        claim(pe, "XT", i, known)
                        transposes("XT", lambda cc, t: xn[:, t, cc * P:(cc + 1) * P])
                    if k == 6 and has(0, i, known):
                        pe.wait_ge(av_ready[0], i + 1)
                        claim(pe, "C1T", i, known)
                        transposes("C1T", lambda q, gg: av[:, 0, gg, q * P:(q + 1) * P])
                    if has(0, i, known):
                        logits_by_key(2 * k)
                    if k == 2 and has(-1, i, known):
                        pe.wait_ge(took["C2T"], i)
                        claim(pe, "NT", i, known)
                        transposes("NT", lambda cc, t: an[:, t, cc * P:(cc + 1) * P])
                    if k == 5 and has(3, i, known):
                        pe.wait_ge(xnT_ready, i + 4)
                        claim(pe, "Q", i, known)
                        product("Q", lambda u, cc, n: w_part[:, WEIGHT["Q"], u, cc, n * P:(n + 1) * P], lambda u, cc, n: xnT[:, u, cc, :])
                    if has(1, i, known):
                        logits_by_query(2 * k)
                    if k == 0 and has(0, i, known):
                        negmax("MTb", 1, i, i, known)
                    if k == 1 and has(-1, i, known):
                        pe.wait_ge(av_ready[1], i)
                        claim(pe, "C2T", i, known)
                        transposes("C2T", lambda q, gg: av[:, 1, gg, q * P:(q + 1) * P])
                    if k == 3 and has(-1, i, known):
                        pe.wait_ge(took["NT"], i)
                        if known == 1:
                            pe.wait_ge(bias_ready, 3)
                        claim(pe, "O", i, known)
                        product("O", lambda u, cc, n: anT[:, u, cc, n * P:(n + 1) * P], lambda u, cc, n: w_part[:, WEIGHT["O"], u, cc, :])
                    if has(0, i, known):
                        logits_by_key(2 * k + 1)
                    if k == 0 and has(-1, i, known):
                        times_v(i - 1, known, QUADS - 1, slot_of(slot, -1))
                    if k == 4 and has(1, i, known):
                        negmax("MTa", 0, i + 1, i, known)
                    if has(1, i, known):
                        logits_by_query(2 * k + 1)
                    if k == 6 and has(-1, i, known):
                        pe.wait_ge(took["X2T"], i)
                        claim(pe, "R", i, known)
                        for t in range(TC):
                            for cc in range(KC):
                                r = t_.matmul(bank_of("R")[:, t * E:(t + 1) * E], x2T[:, cc, t * P:(t + 1) * P], wg_sb[:, cc, :],
                                              start=(cc == 0), stop=(cc == KC - 1))
                        r.then_inc(made["R"], 1)
                    if k == 7 and has(1, i, known):
                        claim(pe, "V", i, known)
                        product("V", lambda u, cc, n: cT[:, s1, u, cc, n * P:(n + 1) * P], lambda u, cc, n: w_part[:, WEIGHT["V"], u, cc, :])
                    if k > 0 and has(0, i, known):
                        times_v(i, known, k - 1, slot)
                    if k == 0 and has(3, i, known):
                        pe.wait_ge(c_landed[s3], 16 * rnd(3))
                        claim(pe, "CT", i, known)
                        transposes("CT", lambda cc, t: c_sb[:, s3, t, cc * P:(cc + 1) * P])
                    if known == B:
                        if k == 0:
                            pe.wait_ge(we_landed, 32)
                        if k >= 4:
                            pe.wait_ge(weT_ready, k - 3)
                        for c in range(KC):
                            for f in range(KC):
                                r = t_.transpose(we_bank(k)[:, c * D + f * P:c * D + (f + 1) * P],
                                                 w_in[:, k, f, c * P:(c + 1) * P], ident[:, :])
                        r.then_inc(we_T, 1)
                    if k == 1 and has(3, i, known):
                        if known == -3:
                            pe.wait_ge(w_low, 2)
                        pe.wait_ge(took["CT"], i + 4)
                        claim(pe, "K", i, known)
                        product("K", lambda u, cc, n: w_part[:, WEIGHT["K"], u, cc, n * P:(n + 1) * P], lambda u, cc, n: cT[:, s3, u, cc, :])
                    if k == 5 and has(-1, i, known):
                        pe.wait_ge(x2n_ready, i)
                        claim(pe, "X2T", i, known)
                        transposes("X2T", lambda cc, t: x2n[:, t, cc * P:(cc + 1) * P])
                    if k == 7 and has(-1, i, known):
                        pe.wait_ge(route, ROUTE * (i - 1) + ROUTE1)
                        claim(pe, "L", i, known)
                        o = bank_of("L")[:, 0:TC * E]
                        t_.matmul(o, tri[:, :], oh[:, :, :].rearrange("p q e -> p (q e)"), start=True, stop=False)
                        t_.matmul(o[:, E:TC * E], onesm[:, :], oh[:, 0, :], start=False, stop=False)
                        pe.wait_ge(seen_ready, TC * i)
                        for t in range(TC):
                            r = t_.matmul(o[:, t * E:(t + 1) * E], onesm[:, :], seen[:, :], start=False, stop=(t == TC - 1))
                        r.then_inc(made["L"], 1)

            looped(pe, turn)

            def slots_T(e, r):
                if e >= 1:
                    pe.wait_ge(gT_ready, 2 * (e - 1) + r + 1)
                for q in range(2):
                    pe.wait_ge(gn_ready, GT * e + 2 * r + q + 1)
                    for c in range(KC):
                        o = t_.transpose(P1[r][:, c * S + q * P:c * S + (q + 1) * P],
                                         g_n[:, e % 2, 2 * r + q, c * P:(c + 1) * P], ident[:, :])
                o.then_inc(gT_made, 1)

            pe.wait_ge(weT_ready, E)
            for r in range(2):
                slots_T(0, r)
            for e in range(E):
                for r in range(2):
                    pe.wait_ge(gT_ready, 2 * e + r + 1)
                    if e >= 2:
                        pe.wait_ge(y_chain, 4 * (e - 2) + 2 * r + 1)
                    for q in range(2):
                        for c in range(KC):
                            o = t_.matmul(g_bank(e, r)[:, q * D:(q + 1) * D], g_T[:, e % 2, r, c, q * P:(q + 1) * P],
                                          weT[:, e, c, :], start=(c == 0), stop=(c == KC - 1))
                    o.then_inc(y_made, 1)
                    if e + 1 < E:
                        slots_T(e + 1, r)


_INS = ["x", "ctx_1024", "mask_Bx1x1xS2_ik0", "L0_xattn_Wq", "L0_xattn_bq", "L0_xattn_Wk", "L0_xattn_bk",
        "L0_xattn_Wv", "L0_xattn_bv", "L0_xattn_Wo", "L0_xattn_bo", "L0_ffn_wg", "L0_ffn_W", "L0_ffn_b"]


def kernel(**inputs):
    import numpy as _np
    import concourse.bacc as _bacc
    from concourse import mybir as _mybir
    from concourse.bass_utils import run_bass_kernel_spmd as _run

    nc = _bacc.Bacc("TRN2", target_bir_lowering=False, num_devices=1)
    arrays, args = {}, []
    for name in _INS:
        a = _np.ascontiguousarray(inputs[name])
        arrays[f"in_{name}"] = a
        args.append(nc.dram_tensor(f"in_{name}", a.shape, _mybir.dt.from_np(a.dtype), kind="ExternalInput").ap())
    shape = inputs["x"].shape
    out = nc.dram_tensor("out_0", shape, _mybir.dt.float32, kind="ExternalOutput").ap()
    xattn_moe(nc, *args, out)
    r = _run(nc, [arrays], core_ids=[0])
    return r.results[0]["out_0"]
```
